# Optimizing a Trainium2 kernel written in Bass

```python
import numpy as np
import jax
import jax.numpy as jnp

def _softmax(x, axis=-1):
    return jax.nn.softmax(x, axis=axis)

def _gelu(x):
    return jax.nn.gelu(x, approximate=True)

def _silu(x):
    return jax.nn.silu(x)

def _sigmoid(x):
    return jax.nn.sigmoid(x)

def _layernorm(x, axis=-1, eps=1e-05):
    m = jnp.mean(x, axis=axis, keepdims=True)
    v = jnp.var(x, axis=axis, keepdims=True)
    return (x - m) / jnp.sqrt(v + eps)

def _scatter_add(tgt, idx, src, axis=0):
    return tgt.at[idx].add(src)

def _segment_sum(src, seg, n):
    return jax.ops.segment_sum(src, seg, n)
kernel_name = 'mk_xattn_ffn_d1_seqx_r8_b4ca40'

def setup_inputs(seed: int=0):
    np.random.seed(seed)
    _w = jnp.asarray

    def _rec_inputs():
        import jax
        import jax.numpy as jnp
        _rk = jax.random.key(seed)
        x = 7.22e-05 + 1 * jax.random.normal(jax.random.fold_in(_rk, 1), (4, 256, 256), jnp.float32)
        _lenS = 256 - jax.random.randint(jax.random.fold_in(_rk, 7), (4,), 0, max(1, 256 // 4) + 1, jnp.int32)
        _lenS2 = 256 - jax.random.randint(jax.random.fold_in(_rk, 8), (4,), 0, max(1, 256 // 4) + 1, jnp.int32)
        _ctx_1024P = jax.random.normal(jax.random.fold_in(_rk, 11), (4, 16, 128), jnp.float32)
        _ctx_1024c = jax.random.dirichlet(jax.random.fold_in(_rk, 511), 0.3 * jnp.ones((16,), jnp.float32), (4, 256))
        _ctx_1024t = jnp.einsum('bsk,bkd->bsd', _ctx_1024c, _ctx_1024P)
        _ctx_1024t = _ctx_1024t * jax.lax.rsqrt(jnp.mean(jnp.square(_ctx_1024t)) + 1e-12) * 0.953939
        ctx_1024 = 2.81802e-05 + 1.00001 * (_ctx_1024t + 0.3 * jax.random.normal(jax.random.fold_in(_rk, 611), (4, 256, 128), jnp.float32))
        return (x, ctx_1024)
    x, ctx_1024 = _rec_inputs()

    def _L0_xattn_setup():
        import jax, jax.numpy as jnp
        import numpy as np
        key = jax.random.key(seed)
        ks = jax.random.split(key, 6)
        B, L, N, C, D = (8, 64, 256, 128, 128)
        return {'teacher_logits': jax.random.normal(ks[0], (B, L, N), dtype=jnp.float32), 'teacher_features': jax.random.normal(ks[1], (B, N, C), dtype=jnp.float32), 'Wq': jax.random.normal(ks[2], (D, C), dtype=jnp.float32) * (1.0 / np.sqrt(C)), 'bq': jnp.zeros((D,), dtype=jnp.float32), 'Wk': jax.random.normal(ks[3], (D, C), dtype=jnp.float32) * (1.0 / np.sqrt(C)), 'bk': jnp.zeros((D,), dtype=jnp.float32)}
    _L0_xattn_all = _L0_xattn_setup()
    _L0_xattn_in = {k: v for k, v in _L0_xattn_all.items() if k in ('Wq', 'bq', 'Wk', 'bk')}
    del _L0_xattn_all

    def _L0_ffn_setup():
        import jax, jax.numpy as jnp
        import numpy as np
        FP8_MAX = 448.0
        GLOBAL_DIV = 448.0 * 6.0

        def _fp8(x):
            return x.astype(jnp.float8_e4m3fn).astype(jnp.float32)

        def _reorder_quantize_x(x, idx):
            scale = jnp.max(jnp.abs(x)) / GLOBAL_DIV
            xr = (x / scale)[:, idx]
            scale_x = jnp.max(jnp.abs(xr), axis=1, keepdims=True) / FP8_MAX
            qx = _fp8(xr / scale_x)
            return (qx, scale_x, scale)

        def _qlinear(qx, scale_x, scale, W, idx, out_idx=None):
            Wr = W[:, idx]
            w_scale = jnp.max(jnp.abs(Wr), axis=1, keepdims=True) / FP8_MAX
            qw = _fp8(Wr / w_scale)
            y = qx * scale_x @ (qw * w_scale).T * scale
            if out_idx is not None:
                y = y[:, out_idx]
            return y
        key = jax.random.key(seed)
        ks = jax.random.split(key, 6)
        B, S, H, I = (2, 128, 256, 704)
        return {'x': jax.random.normal(ks[0], (B, S, H), jnp.float32), 'w_gate': jax.random.normal(ks[1], (I, H), jnp.float32) * 0.02, 'w_up': jax.random.normal(ks[2], (I, H), jnp.float32) * 0.02, 'w_down': jax.random.normal(ks[3], (H, I), jnp.float32) * 0.02, 'up_reorder_index': jax.random.permutation(ks[4], jnp.arange(H, dtype=jnp.int64)), 'down_reorder_index': jax.random.permutation(ks[5], jnp.arange(I, dtype=jnp.int64))}
    _L0_ffn_all = _L0_ffn_setup()
    _L0_ffn_in = {k: v for k, v in _L0_ffn_all.items() if k in ('w_gate', 'w_up', 'w_down', 'up_reorder_index', 'down_reorder_index')}
    del _L0_ffn_all
    return {'x': x, 'ctx_1024': ctx_1024, 'L0_xattn_Wq': _L0_xattn_in['Wq'], 'L0_xattn_bq': _L0_xattn_in['bq'], 'L0_xattn_Wk': _L0_xattn_in['Wk'], 'L0_xattn_bk': _L0_xattn_in['bk'], 'L0_ffn_w_gate': _L0_ffn_in['w_gate'], 'L0_ffn_w_up': _L0_ffn_in['w_up'], 'L0_ffn_w_down': _L0_ffn_in['w_down'], 'L0_ffn_up_reorder_index': _L0_ffn_in['up_reorder_index'], 'L0_ffn_down_reorder_index': _L0_ffn_in['down_reorder_index']}

def reference(x, ctx_1024, L0_xattn_Wq, L0_xattn_bq, L0_xattn_Wk, L0_xattn_bk, L0_ffn_w_gate, L0_ffn_w_up, L0_ffn_w_down, L0_ffn_up_reorder_index, L0_ffn_down_reorder_index):
    import jax
    import jax.numpy as jnp

    def _L0_xattn_ref(teacher_logits, teacher_features, Wq, bq, Wk, bk):
        import jax, jax.numpy as jnp
        import numpy as np
        query = jnp.einsum('bnc,dc->bnd', teacher_features, Wq) + bq
        key = jnp.einsum('bnc,dc->bnd', teacher_features, Wk) + bk
        energy = jnp.einsum('bnd,bmd->bnm', query, key)
        attention = jax.nn.softmax(energy, axis=-1)
        x_m = jnp.einsum('bln,bmn->blm', teacher_logits, attention)
        return x_m

    def _L0_ffn_ref(x, w_gate, w_up, w_down, up_reorder_index, down_reorder_index):
        import jax, jax.numpy as jnp
        import numpy as np
        FP8_MAX = 448.0
        GLOBAL_DIV = 448.0 * 6.0

        def _fp8(x):
            return x.astype(jnp.float8_e4m3fn).astype(jnp.float32)

        def _reorder_quantize_x(x, idx):
            scale = jnp.max(jnp.abs(x)) / GLOBAL_DIV
            xr = (x / scale)[:, idx]
            scale_x = jnp.max(jnp.abs(xr), axis=1, keepdims=True) / FP8_MAX
            qx = _fp8(xr / scale_x)
            return (qx, scale_x, scale)

        def _qlinear(qx, scale_x, scale, W, idx, out_idx=None):
            Wr = W[:, idx]
            w_scale = jnp.max(jnp.abs(Wr), axis=1, keepdims=True) / FP8_MAX
            qw = _fp8(Wr / w_scale)
            y = qx * scale_x @ (qw * w_scale).T * scale
            if out_idx is not None:
                y = y[:, out_idx]
            return y
        B, S, H = x.shape
        xf = x.reshape(B * S, H)
        qx, sx, sc = _reorder_quantize_x(xf, up_reorder_index)
        g = _qlinear(qx, sx, sc, w_gate, up_reorder_index, out_idx=down_reorder_index)
        u = _qlinear(qx, sx, sc, w_up, up_reorder_index, out_idx=down_reorder_index)
        t = jax.nn.silu(g) * u
        qt, st, sct = _reorder_quantize_x(t, down_reorder_index)
        y = _qlinear(qt, st, sct, w_down, down_reorder_index)
        return y.reshape(B, S, H)
    x = x + _L0_xattn_ref(_layernorm(x, axis=-1), ctx_1024, L0_xattn_Wq, L0_xattn_bq, L0_xattn_Wk, L0_xattn_bk)
    x = x + _L0_ffn_ref(_layernorm(x, axis=-1), L0_ffn_w_gate, L0_ffn_w_up, L0_ffn_w_down, L0_ffn_up_reorder_index, L0_ffn_down_reorder_index)
    return x

_drawn_inputs = setup_inputs


def setup_inputs(seed=0):
    import zlib

    import numpy as np

    out = dict(_drawn_inputs(seed))
    spreads = {'L0_xattn_bq': (0.0, 0.1), 'L0_xattn_bk': (0.0, 0.1)}
    factors = {}
    for name, (base, spread) in spreads.items():
        noise = np.random.default_rng([zlib.crc32(name.encode()), seed]).standard_normal(out[name].shape)
        drawn = base * np.exp(spread * noise) if base else spread * noise
        out[name] = jnp.asarray(drawn.astype(out[name].dtype))
    for name, factor in factors.items():
        out[name] = (out[name] * factor).astype(out[name].dtype)
    return out
```

```python
from contextlib import ExitStack

import concourse.bass as bass
from concourse import mybir

P = 128
F32 = mybir.dt.float32
BF16 = mybir.dt.bfloat16
U16 = mybir.dt.uint16
I32 = mybir.dt.int32
U32 = mybir.dt.uint32
ALU = mybir.AluOpType
ACT = mybir.ActivationFunctionType
AX_X = mybir.AxisListType.X

FP8_MAX = 448.0
LN_EPS = 1e-5
GRID_SHIFT = 20
LEAST = 1.5 * 2.0 ** (GRID_SHIFT - 6)
EXPONENT_BITS = 0x7F80
HALF_BIT = 0x0040


def build(nc, x, ctx_t, wqk, w_gate_up, w_down, down_idx_a, down_idx_b, out):
    B, L, N = x.shape
    C = ctx_t.shape[0]
    I = w_gate_up.shape[0]
    LT = L // P
    NC = N // P
    T = B * LT
    KC = -(-I // P)
    rows = [min(P, I - P * k) for k in range(KC)]
    rows_and_down = rows + [P]

    def hidden_cols(k):
        return slice(k * P + rows[k] - P, k * P + rows[k])

    IH = I // 2
    HB = B // 2
    assert L == N and C == P and LT == 2 and NC == 2 and T % 2 == 0

    with ExitStack() as ctx:
        def sb(name, shape, dt=F32):
            return ctx.enter_context(nc.sbuf_tensor(name, shape, dt))

        def sem(name):
            return ctx.enter_context(nc.semaphore(name))

        wqk_sb = sb("wqk_sb", [P, 2 * P + 2])
        ctx_sb = sb("ctx_sb", [P, B * N])
        x_sb = sb("x_sb", [P, B, LT, N])
        idx_sb = sb("idx_sb", [P, KC], I32)
        wup_sb = sb("wup_sb", [P, KC, 2, N])
        wdn_sb = sb("wdn_sb", [P, NC, I])
        ident = sb("ident", [P, P])
        identb = sb("identb", [P, P], BF16)
        ones = sb("ones", [P, P])
        scale_consts = sb("scale_consts", [P, 2])
        minus_half = sb("minus_half", [P, 2])

        qT = sb("qT", [P, B * N])
        kT = sb("kT", [P, B * N])
        xc = sb("xc", [P, B, LT, N])
        xcT = sb("xcT", [P, B, NC, L])
        neg_max = sb("neg_max", [P, B, 2])
        expd = sb("expd", [P, B, 2, N])
        z = sb("z", [P, B, 2])
        rz = sb("rz", [P, B, 2])
        att = sb("att", [P, B, 2, N])
        attT = sb("attT", [P, B, NC, N])
        x1 = sb("x1", [P, B, LT, N])
        st1 = sb("st1", [P, T, 6])
        mv1 = sb("mv1", [P, T, 2])
        ve1 = sb("ve1", [P, T])
        rstd1 = sb("rstd1", [P, T])
        st2 = sb("st2", [P, T, 6])
        mv2 = sb("mv2", [P, T, 2])
        ve2 = sb("ve2", [P, T])
        rstd2 = sb("rstd2", [P, T])
        xc2 = sb("xc2", [P, B, LT, N])
        amax_x = sb("amax_x", [P, T])
        rec_x = sb("rec_x", [P, T])
        s_x = sb("s_x", [P, T, 2])
        rowscale = sb("rowscale", [P, T])
        mag_x = sb("mag_x", [P, LT, N], BF16)
        sum_x = sb("sum_x", [P, LT, N])
        q_x = sb("q_x", [P, B, LT, N], BF16)
        qxT = sb("qxT", [P, B, NC, L], BF16)

        amax_w = sb("amax_w", [P, KC, 2])
        rec_w = sb("rec_w", [P, KC, 2])
        s_w = sb("s_w", [P, KC, 2, 2])
        mag_w = sb("mag_w", [P, 2, N], BF16)
        sum_w = sb("sum_w", [P, 2, N])
        q_w = sb("q_w", [P, KC, 2, N], BF16)
        wupT = sb("wupT", [P, NC, 2, I], BF16)
        amax_d = sb("amax_d", [P, NC])
        rec_d = sb("rec_d", [P, NC])
        s_d = sb("s_d", [P, NC, 2])
        mag_d = sb("mag_d", [P, I], BF16)
        sum_d = sb("sum_d", [P, I])
        q_d = sb("q_d", [P, NC, I], BF16)
        wdnT = sb("wdnT", [P, KC, N], BF16)
        diag = sb("diag", [P, 2, 2, P])
        wup_scale = sb("wup_scale", [P, 2, I])
        wdn_scale = sb("wdn_scale", [P, N])

        g_sb = sb("g_sb", [P, 2, I])
        act_g = sb("act_g", [P, 2, I])
        act_ws = sb("act_ws", [P, 2, I])
        t_sb = sb("t_sb", [P, 2, I])
        amax_t = sb("amax_t", [P, T])
        rec_t = sb("rec_t", [P, T])
        s_t = sb("s_t", [P, T, 2])
        yscale = sb("yscale", [P, T])
        mag_t = sb("mag_t", [P, 2, I], BF16)
        sum_t = sb("sum_t", [P, 2, I])
        q_t = sb("q_t", [P, 2, I], BF16)
        tT = sb("tT", [P, 2, KC, P], BF16)
        y_sb = sb("y_sb", [P, 2, N])
        o_sb = sb("o_sb", [P, T, N])

        bank = [ctx.enter_context(nc.psum_tensor(f"bank{n}", [P, 512], F32)) for n in range(2)]
        gate_ps = ctx.enter_context(nc.psum_tensor("gate_ps", [P, 2, 512], F32))
        up_ps = ctx.enter_context(nc.psum_tensor("up_ps", [P, 2, 512], F32))
        bank67 = [ctx.enter_context(nc.psum_tensor(f"bank{n}", [P, 512], F32)) for n in (6, 7)]
        proj_ps = bank
        wT_ps = bank[0][:, :].bitcast(BF16)
        tT_ps = bank[1][:, :].bitcast(BF16)
        bc_ps = bank[1][:, 0:2 * P].rearrange("p (a n) -> p a n", a=2)
        scores_ps = [gate_ps[:, n, :].rearrange("p (j n) -> p j n", j=2) for n in range(2)]
        attT_ps = up_ps[:, 0, :].rearrange("p (j n) -> p j n", j=2)
        xcT_ps = up_ps[:, 1, :].rearrange("p (j n) -> p j n", j=2)
        xm_ps = bank67[0][:, :].rearrange("p (j n) -> p j n", j=2)
        qxT_ps = bank67[1][:, :].bitcast(BF16)[:, 0:NC * L].rearrange("p (j n) -> p j n", j=2)
        y_ps = [bank67[n][:, 0:N] for n in range(2)]

        wqk_in = sem("wqk_in")
        ctx_in = [sem(f"ctx_in{h}") for h in range(2)]
        x_in = [sem(f"x_in{h}") for h in range(2)]
        idx_in = sem("idx_in")
        wup_in = [sem(f"wup_in{k}") for k in range(KC)]
        wdn_in = sem("wdn_in")
        out_done = sem("out_done")
        proj_ready = sem("proj_ready")
        scores_ready = sem("scores_ready")
        xcT_ready = sem("xcT_ready")
        attT_ready = sem("attT_ready")
        xm_ready = sem("xm_ready")
        qxT_ready = sem("qxT_ready")
        wT_ready = sem("wT_ready")
        bc_ready = sem("bc_ready")
        gate_ready = sem("gate_ready")
        up_ready = sem("up_ready")
        tT_ready = sem("tT_ready")
        y_ready = sem("y_ready")
        q_evac = sem("q_evac")
        exp_done = sem("exp_done")
        xcT_evac = sem("xcT_evac")
        attT_evac = sem("attT_evac")
        bc_evac = sem("bc_evac")
        silu_done = sem("silu_done")
        tT_evac = sem("tT_evac")
        dve_step = sem("dve_step")
        k_evac = sem("k_evac")
        var1_done = sem("var1_done")
        xc_done = sem("xc_done")
        max_done = sem("max_done")
        rz_done = sem("rz_done")
        x1_done = sem("x1_done")
        var2_done = sem("var2_done")
        amax_x_done = sem("amax_x_done")
        q_x_done = sem("q_x_done")
        qxT_evac = sem("qxT_evac")
        q_w_done = sem("q_w_done")
        wT_evac = sem("wT_evac")
        diag_done = sem("diag_done")
        gate_scaled = sem("gate_scaled")
        t_done = sem("t_done")
        amax_t_done = sem("amax_t_done")
        sum_t_done = sem("sum_t_done")
        y_scaled = sem("y_scaled")
        pool_step = sem("pool_step")
        consts_ready = sem("consts_ready")
        rstd1_done = sem("rstd1_done")
        att_done = sem("att_done")
        rstd2_done = sem("rstd2_done")
        ws_done = sem("ws_done")
        q_t_done = sem("q_t_done")
        out_ready = sem("out_ready")

        block = ctx.enter_context(nc.Block())

        @block.sync
        def _(sp):
            sp.dma_start(wqk_sb[:, :], wqk).then_inc(wqk_in, 16)
            sp.dma_start(ctx_sb[:, 0:HB * N], ctx_t[:, 0:HB * N]).then_inc(ctx_in[0], 16)
            sp.dma_start(idx_sb[:, 0:KC - 1], down_idx_a).then_inc(idx_in, 16)
            sp.dma_start(idx_sb[0:rows[-1], KC - 1:KC], down_idx_b).then_inc(idx_in, 16)
            xv = x.rearrange("b (j p) n -> p b j n", p=P)
            sp.dma_start(x_sb[:, 0:HB], xv[:, 0:HB]).then_inc(x_in[0], 16)
            sp.dma_start(ctx_sb[:, HB * N:], ctx_t[:, HB * N:]).then_inc(ctx_in[1], 16)
            sp.dma_start(x_sb[:, HB:], xv[:, HB:]).then_inc(x_in[1], 16)
            sp.dma_start(wdn_sb[:, :, :], w_down.rearrange("(j p) i -> p j i", p=P)).then_inc(wdn_in, 16)
            ov = out.rearrange("b (j p) n -> (b j) p n", p=P)
            for i in range(T):
                sp.wait_ge(out_ready, i + 1)
                sp.dma_start(ov[i], o_sb[:, i, :]).then_inc(out_done, 16)
            sp.wait_ge(out_done, 16 * T)

        @block.gpsimd
        def _(pool):
            nc.gpsimd.memset(ident[:, :], 0.0).then_inc(pool_step, 1)
            nc.gpsimd.memset(minus_half[:, :], -0.5).then_inc(pool_step, 1)
            pool.wait_ge(pool_step, 2)
            nc.gpsimd.affine_select(out=ident[:, :], in_=ident[:, :], compare_op=ALU.not_equal, fill=1.0,
                                    base=0, pattern=[[-1, P]], channel_multiplier=1).then_inc(pool_step, 1)
            pool.wait_ge(pool_step, 3)
            nc.gpsimd.tensor_copy(identb[:, :], ident[:, :]).then_inc(consts_ready, 1)
            pool.wait_ge(idx_in, 32)
            for k in range(KC):
                nc.gpsimd.indirect_dma_start(
                    out=wup_sb[0:rows[k], k].rearrange("p a n -> p (a n)"), out_offset=None,
                    in_=w_gate_up,
                    in_offset=bass.IndirectOffsetOnAxis(ap=idx_sb[0:rows[k], k:k + 1], axis=0),
                ).then_inc(wup_in[k], 16)

            def rstd1_of(b):
                pool.wait_ge(var1_done, b + 1)
                nc.gpsimd.tensor_tensor(rstd1[:, 2 * b:2 * b + 2], ve1[:, 2 * b:2 * b + 2], minus_half[:, :],
                                        ALU.pow).then_inc(rstd1_done, 1)

            def normalise(b):
                pool.wait_ge(rz_done, b + 1)
                for j in range(2):
                    last = nc.gpsimd.tensor_scalar(att[:, b, j], expd[:, b, j], rz[:, b, j:j + 1], 1.0,
                                                   ALU.mult, ALU.mult)
                last.then_inc(att_done, 1)

            def rowscale_of(b):
                pair = slice(2 * b, 2 * b + 2)
                pool.wait_ge(var2_done, b + 1)
                nc.gpsimd.tensor_tensor(rstd2[:, pair], ve2[:, pair], minus_half[:, :],
                                        ALU.pow).then_inc(pool_step, 1)
                pool.wait_ge(pool_step, 4 + b)
                pool.wait_ge(amax_x_done, b + 1)
                nc.gpsimd.tensor_tensor(rowscale[:, pair], rstd2[:, pair], amax_x[:, pair],
                                        ALU.mult).then_inc(rstd2_done, 1)
            for b in range(B):
                rstd1_of(b)
            for b in range(B):
                normalise(b)
                if b >= 1:
                    rowscale_of(b - 1)
            rowscale_of(B - 1)
            for i in range(T + 2):
                if i < T:
                    pool.wait_ge(silu_done, i + 1)
                    pool.wait_ge(bc_evac, 2 * KC)
                    nc.gpsimd.tensor_tensor(act_ws[:, i % 2], act_g[:, i % 2], wup_scale[:, 1],
                                            ALU.mult).then_inc(ws_done, 1)
                if 1 <= i <= T:
                    pool.wait_ge(sum_t_done, i)
                    if i >= 3:
                        pool.wait_ge(tT_ready, i - 2)
                    nc.gpsimd.tensor_tensor(q_t[:, (i - 1) % 2], sum_t[:, (i - 1) % 2], mag_t[:, (i - 1) % 2],
                                            ALU.subtract).then_inc(q_t_done, 1)
                if i >= 2:
                    pool.wait_ge(y_scaled, i - 1)
                    nc.gpsimd.tensor_tensor(o_sb[:, i - 2], y_sb[:, i % 2], x1[:, (i - 2) // 2, i % 2],
                                            ALU.add).then_inc(out_ready, 1)

        @block.scalar
        def _(act):
            def evac_q(h):
                act.wait_ge(wqk_in, 16)
                act.wait_ge(proj_ready, 2 * h + 1)
                nc.scalar.activation(qT[:, h * HB * N:(h + 1) * HB * N], proj_ps[0][:, :], ACT.Identity,
                                     bias=wqk_sb[:, 2 * P:2 * P + 1]).then_inc(q_evac, 1)

            def exps(b):
                act.wait_ge(max_done, b + 1)
                for j in range(2):
                    last = nc.scalar.activation(expd[:, b, j], scores_ps[b % 2][:, j], ACT.Exp,
                                                bias=neg_max[:, b, j:j + 1], accum_out=z[:, b, j:j + 1])
                    last.then_inc(exp_done, 1)

            def evac_xcT(b):
                act.wait_ge(xcT_ready, b + 1)
                nc.scalar.activation(xcT[:, b], xcT_ps, ACT.Copy).then_inc(xcT_evac, 1)

            def evac_attT(b):
                act.wait_ge(attT_ready, b + 1)
                nc.scalar.activation(attT[:, b], attT_ps, ACT.Copy).then_inc(attT_evac, 1)

            def evac_scales(k):
                r = rows_and_down[k]
                act.wait_ge(bc_ready, k + 1)
                for a in range(2):
                    if k < KC:
                        dst, factor = wup_scale[:, a, k * P:k * P + r], (FP8_MAX ** -2, 1.0 / FP8_MAX)[a]
                    else:
                        dst, factor = wdn_scale[:, a * P:(a + 1) * P], 1.0 / FP8_MAX
                    nc.scalar.activation(dst, bc_ps[:, a, 0:r], ACT.Copy, scale=factor).then_inc(bc_evac, 1)

            evac_q(0)
            evac_q(1)
            evac_xcT(0)
            exps(0)
            exps(1)
            evac_attT(0)
            evac_xcT(1)
            exps(2)
            evac_attT(1)
            evac_xcT(2)
            exps(3)
            evac_attT(2)
            evac_xcT(3)
            evac_scales(0)
            evac_attT(3)
            for k in range(1, KC + 1):
                evac_scales(k)
            for i in range(T + 1):
                if i < T:
                    act.wait_ge(gate_scaled, i + 1)
                    act.wait_ge(rstd2_done, i // 2 + 1)
                    if i >= 2:
                        act.wait_ge(ws_done, i - 1)
                    nc.scalar.activation(act_g[:, i % 2], g_sb[:, i % 2], ACT.Silu,
                                         scale=rowscale[:, i:i + 1]).then_inc(silu_done, 1)
                if i >= 1:
                    act.wait_ge(tT_ready, i)
                    if i >= 3:
                        act.wait_ge(y_ready, i - 2)
                    nc.scalar.activation(tT[:, (i - 1) % 2], tT_ps[:, 0:KC * P].rearrange("p (k n) -> p k n", k=KC),
                                         ACT.Copy).then_inc(tT_evac, 1)

        @block.vector
        def _(dve):
            steps = [0]

            def step(ins):
                ins.then_inc(dve_step, 1)
                steps[0] += 1
                return steps[0]

            def evac_k(h):
                dve.wait_ge(wqk_in, 16)
                dve.wait_ge(proj_ready, 2 * h + 2)
                nc.vector.tensor_scalar(kT[:, h * HB * N:(h + 1) * HB * N], proj_ps[1][:, :],
                                        wqk_sb[:, 2 * P + 1:2 * P + 2], None, ALU.add).then_inc(k_evac, 1)

            def centre_x(b):
                dve.wait_ge(x_in[b // HB], 16)
                for j in range(2):
                    n = step(nc.vector.bn_stats(st1[:, 2 * b + j], x_sb[:, b, j]))
                dve.wait_ge(dve_step, n)
                for j in range(2):
                    n = step(nc.vector.bn_aggr(mv1[:, 2 * b + j], st1[:, 2 * b + j]))
                dve.wait_ge(dve_step, n)
                nc.vector.tensor_scalar(ve1[:, 2 * b:2 * b + 2], mv1[:, 2 * b:2 * b + 2, 1], LN_EPS, None,
                                        ALU.add).then_inc(var1_done, 1)
                for j in range(2):
                    last = nc.vector.tensor_scalar(xc[:, b, j], x_sb[:, b, j], mv1[:, 2 * b + j, 0:1], None,
                                                   ALU.subtract)
                last.then_inc(xc_done, 1)

            def score_max(b):
                dve.wait_ge(scores_ready, b + 1)
                nc.vector.tensor_reduce(neg_max[:, b], scores_ps[b % 2], AX_X, ALU.max,
                                        negate=True).then_inc(max_done, 1)

            def recip_z(b):
                dve.wait_ge(exp_done, 2 * b + 2)
                nc.vector.reciprocal(rz[:, b], z[:, b]).then_inc(rz_done, 1)

            def quantize(src, scales, mag, total, join):
                for s, sc, m in zip(src, scales, mag):
                    n = step(nc.vector.tensor_scalar(m, s, sc[:, 1:2], None, ALU.mult))
                dve.wait_ge(dve_step, n)
                bits = join.bitcast(U16)
                n = step(nc.vector.tensor_scalar(bits, bits, EXPONENT_BITS, HALF_BIT, ALU.bitwise_and,
                                                 ALU.bitwise_or))
                dve.wait_ge(dve_step, n)
                n = step(nc.vector.tensor_scalar(join, join, LEAST, None, ALU.max))
                dve.wait_ge(dve_step, n)
                for s, sc, m, w in zip(src, scales, mag, total):
                    last = nc.vector.scalar_tensor_tensor(w, s, sc[:, 0:1], m, ALU.mult, ALU.add)
                return last

            def residual(b):
                dve.wait_ge(xm_ready, b + 1)
                dve.wait_ge(rstd1_done, b + 1)
                for j in range(2):
                    i = 2 * b + j
                    nc.vector.scalar_tensor_tensor(x1[:, b, j], xm_ps[:, j], rstd1[:, i:i + 1],
                                                   x_sb[:, b, j], ALU.mult, ALU.add).then_inc(x1_done, 1)
                dve.wait_ge(x1_done, 2 * b + 2)
                for j in range(2):
                    n = step(nc.vector.bn_stats(st2[:, 2 * b + j], x1[:, b, j]))
                dve.wait_ge(dve_step, n)
                for j in range(2):
                    n = step(nc.vector.bn_aggr(mv2[:, 2 * b + j], st2[:, 2 * b + j]))
                dve.wait_ge(dve_step, n)
                nc.vector.tensor_scalar(ve2[:, 2 * b:2 * b + 2], mv2[:, 2 * b:2 * b + 2, 1], LN_EPS, None,
                                        ALU.add).then_inc(var2_done, 1)
                for j in range(2):
                    n = step(nc.vector.tensor_scalar(xc2[:, b, j], x1[:, b, j], mv2[:, 2 * b + j, 0:1], None,
                                                     ALU.subtract))
                dve.wait_ge(dve_step, n)
                nc.vector.tensor_reduce(amax_x[:, 2 * b:2 * b + 2], xc2[:, b], AX_X, ALU.max,
                                        apply_absolute_value=True).then_inc(amax_x_done, 1)
                dve.wait_ge(amax_x_done, b + 1)
                n = step(nc.vector.reciprocal(rec_x[:, 2 * b:2 * b + 2], amax_x[:, 2 * b:2 * b + 2]))
                dve.wait_ge(dve_step, n)
                for j in range(2):
                    n = step(nc.vector.tensor_scalar(s_x[:, 2 * b + j], scale_consts[:, :],
                                                     rec_x[:, 2 * b + j:2 * b + j + 1], None, ALU.mult))
                dve.wait_ge(dve_step, n)

            def quantize_x(b):
                last = quantize([xc2[:, b, j] for j in range(2)], [s_x[:, 2 * b + j] for j in range(2)],
                                [mag_x[:, j] for j in range(2)], [sum_x[:, j] for j in range(2)],
                                mag_x[:, :, :])
                n = step(last)
                dve.wait_ge(dve_step, n)
                nc.vector.tensor_tensor(q_x[:, b], sum_x[:, :, :], mag_x[:, :, :], ALU.subtract)\
                    .then_inc(q_x_done, 1)

            def evac_qxT(b):
                dve.wait_ge(qxT_ready, b + 1)
                nc.vector.tensor_copy(qxT[:, b], qxT_ps).then_inc(qxT_evac, 1)

            def quantize_up(k):
                r = rows[k]
                dve.wait_ge(wup_in[k], 16)
                n = step(nc.vector.tensor_reduce(amax_w[0:r, k], wup_sb[0:r, k], AX_X, ALU.max,
                                                 apply_absolute_value=True))
                dve.wait_ge(dve_step, n)
                n = step(nc.vector.reciprocal(rec_w[0:r, k], amax_w[0:r, k]))
                dve.wait_ge(dve_step, n)
                for j in range(2):
                    n = step(nc.vector.tensor_scalar(s_w[0:r, k, j], scale_consts[0:r, :], rec_w[0:r, k, j:j + 1],
                                                     None, ALU.mult))
                dve.wait_ge(dve_step, n)
                last = quantize([wup_sb[0:r, k, j] for j in range(2)], [s_w[0:r, k, j] for j in range(2)],
                                [mag_w[0:r, j] for j in range(2)], [sum_w[0:r, j] for j in range(2)],
                                mag_w[0:r, :, :])
                n = step(last)
                dve.wait_ge(dve_step, n)
                nc.vector.tensor_tensor(q_w[0:r, k], sum_w[0:r], mag_w[0:r], ALU.subtract)\
                    .then_inc(q_w_done, 1)

            def evac_wupT(k):
                r = rows[k]
                dve.wait_ge(wT_ready, k + 1)
                nc.vector.tensor_copy(wupT[:, :, :, k * P:k * P + r],
                                      wT_ps[:, 0:4 * P].rearrange("p (c a n) -> p c a n", c=2, a=2)[:, :, :, 0:r])\
                    .then_inc(wT_evac, 1)

            def quantize_down(j):
                dve.wait_ge(wdn_in, 16)
                n = step(nc.vector.tensor_reduce(amax_d[:, j:j + 1], wdn_sb[:, j], AX_X, ALU.max,
                                                 apply_absolute_value=True))
                dve.wait_ge(dve_step, n)
                n = step(nc.vector.reciprocal(rec_d[:, j:j + 1], amax_d[:, j:j + 1]))
                dve.wait_ge(dve_step, n)
                n = step(nc.vector.tensor_scalar(s_d[:, j], scale_consts[:, :], rec_d[:, j:j + 1], None, ALU.mult))
                dve.wait_ge(dve_step, n)
                n = step(quantize([wdn_sb[:, j]], [s_d[:, j]], [mag_d[:, :]], [sum_d[:, :]], mag_d[:, :]))
                dve.wait_ge(dve_step, n)
                nc.vector.tensor_tensor(q_d[:, j], sum_d[:, :], mag_d[:, :], ALU.subtract).then_inc(q_w_done, 1)

            def evac_wdnT(j):
                dve.wait_ge(wT_ready, KC + j + 1)
                src = wT_ps[:, 0:KC * P].rearrange("p (k n) -> p k n", k=KC)
                nc.vector.tensor_copy(wdnT[:, :, j * P:(j + 1) * P], src).then_inc(wT_evac, 1)

            def scale_diagonals(k):
                r = rows_and_down[k]
                if k >= 2:
                    dve.wait_ge(bc_ready, k - 1)
                for a in range(2):
                    peak = amax_w[0:r, k, a:a + 1] if k < KC else amax_d[:, a:a + 1]
                    last = nc.vector.tensor_scalar(diag[0:r, k % 2, a, 0:r], ident[0:r, 0:r], peak, None, ALU.mult)
                last.then_inc(diag_done, 1)

            def gate(i):
                dve.wait_ge(gate_ready, i + 1)
                nc.vector.tensor_tensor(g_sb[:, i % 2].rearrange("p (h n) -> p h n", h=2), gate_ps[:, :, 0:IH],
                                        wup_scale[:, 0].rearrange("p (h n) -> p h n", h=2), ALU.mult)\
                    .then_inc(gate_scaled, 1)

            def hidden(i):
                j = i % 2
                dve.wait_ge(up_ready, i + 1)
                dve.wait_ge(ws_done, i + 1)
                nc.vector.tensor_tensor(t_sb[:, j].rearrange("p (h n) -> p h n", h=2), up_ps[:, :, 0:IH],
                                        act_ws[:, j].rearrange("p (h n) -> p h n", h=2), ALU.mult)\
                    .then_inc(t_done, 1)
                dve.wait_ge(t_done, i + 1)
                nc.vector.tensor_reduce(amax_t[:, i:i + 1], t_sb[:, j], AX_X, ALU.max,
                                        apply_absolute_value=True).then_inc(amax_t_done, 1)
                dve.wait_ge(amax_t_done, i + 1)
                n = step(nc.vector.reciprocal(rec_t[:, i:i + 1], amax_t[:, i:i + 1]))
                dve.wait_ge(rstd2_done, i // 2 + 1)
                step(nc.vector.scalar_tensor_tensor(yscale[:, i:i + 1], amax_t[:, i:i + 1], 1.0 / FP8_MAX ** 2,
                                                    rowscale[:, i:i + 1], ALU.mult, ALU.mult))
                dve.wait_ge(dve_step, n)
                n = step(nc.vector.tensor_scalar(s_t[:, i], scale_consts[:, :], rec_t[:, i:i + 1], None, ALU.mult))
                dve.wait_ge(dve_step, n)
                if i >= 2:
                    dve.wait_ge(q_t_done, i - 1)
                quantize([t_sb[:, j]], [s_t[:, i]], [mag_t[:, j]], [sum_t[:, j]], mag_t[:, j])\
                    .then_inc(sum_t_done, 1)

            def finish(i):
                dve.wait_ge(y_ready, i + 1)
                if i >= 2:
                    dve.wait_ge(out_ready, i - 1)
                nc.vector.scalar_tensor_tensor(y_sb[:, i % 2], y_ps[i % 2], yscale[:, i:i + 1], wdn_scale[:, :],
                                               ALU.mult, ALU.mult).then_inc(y_scaled, 1)

            step(nc.vector.memset(ones[:, :], 1.0))
            step(nc.vector.memset(scale_consts[:, 0:1], FP8_MAX))
            n0 = step(nc.vector.memset(scale_consts[:, 1:2], FP8_MAX * 2.0 ** GRID_SHIFT))
            evac_k(0)
            dve.wait_ge(consts_ready, 1)
            centre_x(0)
            centre_x(1)
            score_max(0)
            evac_k(1)
            score_max(1)
            recip_z(0)
            centre_x(2)
            dve.wait_ge(dve_step, n0)
            quantize_up(0)
            recip_z(1)
            centre_x(3)
            score_max(2)
            residual(0)
            quantize_x(0)
            quantize_up(1)
            score_max(3)
            recip_z(2)
            evac_wupT(0)
            evac_qxT(0)
            residual(1)
            quantize_x(1)
            recip_z(3)
            evac_wupT(1)
            quantize_up(2)
            scale_diagonals(0)
            evac_qxT(1)
            residual(2)
            evac_wupT(2)
            quantize_x(2)
            quantize_up(3)
            scale_diagonals(1)
            evac_qxT(2)
            evac_wupT(3)
            residual(3)
            quantize_x(3)
            quantize_up(4)
            scale_diagonals(2)
            evac_qxT(3)
            evac_wupT(4)
            quantize_up(5)
            scale_diagonals(3)
            quantize_down(0)
            evac_wupT(5)
            quantize_down(1)
            evac_wdnT(0)
            scale_diagonals(4)
            scale_diagonals(5)
            scale_diagonals(KC)
            evac_wdnT(1)
            dve.wait_ge(bc_evac, 2 * KC)
            gate(0)
            dve.wait_ge(bc_evac, 2 * KC + 2)
            for i in range(T):
                if i + 1 < T:
                    gate(i + 1)
                hidden(i)
                if i >= 1:
                    finish(i - 1)
            finish(T - 1)

        @block.tensor
        def _(pe):
            def project(h):
                cols = slice(h * HB * N, (h + 1) * HB * N)
                pe.wait_ge(ctx_in[h], 16)
                if h:
                    pe.wait_ge(q_evac, h)
                nc.tensor.matmul(proj_ps[0][:, :], wqk_sb[:, 0:P], ctx_sb[:, cols], start=True, stop=True)\
                    .then_inc(proj_ready, 1)
                if h:
                    pe.wait_ge(k_evac, h)
                nc.tensor.matmul(proj_ps[1][:, :], wqk_sb[:, P:2 * P], ctx_sb[:, cols], start=True, stop=True)\
                    .then_inc(proj_ready, 1)

            def scores(b):
                pe.wait_ge(q_evac, b // HB + 1)
                pe.wait_ge(k_evac, b // HB + 1)
                if b >= 2:
                    pe.wait_ge(exp_done, 2 * (b - 1))
                for j in range(2):
                    last = nc.tensor.matmul(scores_ps[b % 2][:, j], qT[:, b * N + j * P:b * N + (j + 1) * P],
                                            kT[:, b * N:(b + 1) * N], start=True, stop=True)
                last.then_inc(scores_ready, 1)

            def transpose_xc(b):
                pe.wait_ge(xc_done, b + 1)
                if b:
                    pe.wait_ge(xcT_evac, b)
                for c in range(NC):
                    for j in range(LT):
                        last = nc.tensor.transpose(xcT_ps[:, c, j * P:(j + 1) * P], xc[:, b, j, c * P:(c + 1) * P],
                                                   ident[:, :])
                last.then_inc(xcT_ready, 1)

            def transpose_att(b):
                pe.wait_ge(att_done, b + 1)
                if b:
                    pe.wait_ge(attT_evac, b)
                for c in range(NC):
                    for j in range(2):
                        last = nc.tensor.transpose(attT_ps[:, c, j * P:(j + 1) * P], att[:, b, j, c * P:(c + 1) * P],
                                                   ident[:, :])
                last.then_inc(attT_ready, 1)

            def attend(b):
                pe.wait_ge(xcT_evac, b + 1)
                pe.wait_ge(attT_evac, b + 1)
                if b:
                    pe.wait_ge(x1_done, 2 * b)
                for j in range(LT):
                    for c in range(NC):
                        last = nc.tensor.matmul(xm_ps[:, j], xcT[:, b, c, j * P:(j + 1) * P], attT[:, b, c],
                                                start=(c == 0), stop=(c == NC - 1))
                last.then_inc(xm_ready, 1)

            def transpose_qx(b):
                pe.wait_ge(q_x_done, b + 1)
                if b:
                    pe.wait_ge(qxT_evac, b)
                for c in range(NC):
                    for j in range(LT):
                        last = nc.tensor.transpose(qxT_ps[:, c, j * P:(j + 1) * P], q_x[:, b, j, c * P:(c + 1) * P],
                                                   identb[:, :])
                last.then_inc(qxT_ready, 1)

            def transpose_up(k):
                r = rows[k]
                pe.wait_ge(q_w_done, k + 1)
                if k:
                    pe.wait_ge(wT_evac, k)
                for c in range(NC):
                    for a in range(2):
                        last = nc.tensor.transpose(wT_ps[:, (2 * c + a) * P:(2 * c + a) * P + r],
                                                   q_w[0:r, k, a, c * P:(c + 1) * P], identb[0:r, 0:r])
                last.then_inc(wT_ready, 1)

            def transpose_down(j):
                pe.wait_ge(q_w_done, KC + j + 1)
                pe.wait_ge(wT_evac, KC + j)
                for k in range(KC):
                    last = nc.tensor.transpose(wT_ps[:, k * P:(k + 1) * P], q_d[:, j, hidden_cols(k)],
                                               identb[:, :])
                last.then_inc(wT_ready, 1)

            def spread(k):
                r = rows_and_down[k]
                pe.wait_ge(diag_done, k + 1)
                if k:
                    pe.wait_ge(bc_evac, 2 * k)
                for a in range(2):
                    last = nc.tensor.matmul(bc_ps[:, a, 0:r], ones[0:r, :], diag[0:r, k % 2, a, 0:r],
                                            start=True, stop=True)
                last.then_inc(bc_ready, 1)

            def gates(i):
                b, j = i // LT, i % LT
                if i:
                    pe.wait_ge(gate_scaled, i)
                for h in range(2):
                    for c in range(NC):
                        last = nc.tensor.matmul(gate_ps[:, h, 0:IH], qxT[:, b, c, j * P:(j + 1) * P],
                                                wupT[:, c, 0, h * IH:(h + 1) * IH],
                                                start=(c == 0), stop=(c == NC - 1))
                last.then_inc(gate_ready, 1)

            def ups(i):
                b, j = i // LT, i % LT
                if i:
                    pe.wait_ge(t_done, i)
                for h in range(2):
                    for c in range(NC):
                        last = nc.tensor.matmul(up_ps[:, h, 0:IH], qxT[:, b, c, j * P:(j + 1) * P],
                                                wupT[:, c, 1, h * IH:(h + 1) * IH],
                                                start=(c == 0), stop=(c == NC - 1))
                last.then_inc(up_ready, 1)

            def transpose_t(i):
                pe.wait_ge(q_t_done, i + 1)
                if i:
                    pe.wait_ge(tT_evac, i)
                for k in range(KC):
                    last = nc.tensor.transpose(tT_ps[:, k * P:(k + 1) * P], q_t[:, i % 2, hidden_cols(k)],
                                               identb[:, :])
                last.then_inc(tT_ready, 1)

            def down(i):
                pe.wait_ge(tT_evac, i + 1)
                if i >= 2:
                    pe.wait_ge(y_scaled, i - 1)
                for k in range(KC):
                    last = nc.tensor.matmul(y_ps[i % 2], tT[P - rows[k]:, i % 2, k], wdnT[P - rows[k]:, k],
                                            start=(k == 0), stop=(k == KC - 1))
                last.then_inc(y_ready, 1)

            pe.wait_ge(wqk_in, 16)
            project(0)
            project(1)
            scores(0)
            scores(1)
            pe.wait_ge(consts_ready, 1)
            transpose_xc(0)
            transpose_att(0)
            attend(0)
            transpose_xc(1)
            transpose_up(0)
            scores(2)
            transpose_att(1)
            attend(1)
            transpose_xc(2)
            scores(3)
            transpose_qx(0)
            transpose_up(1)
            transpose_att(2)
            attend(2)
            transpose_xc(3)
            transpose_qx(1)
            transpose_up(2)
            spread(0)
            transpose_att(3)
            attend(3)
            transpose_qx(2)
            transpose_up(3)
            spread(1)
            transpose_qx(3)
            transpose_up(4)
            spread(2)
            transpose_up(5)
            spread(3)
            transpose_down(0)
            transpose_down(1)
            for k in range(4, KC + 1):
                spread(k)
            pe.wait_ge(wT_evac, KC)
            pe.wait_ge(exp_done, 2 * B)
            pe.wait_ge(qxT_evac, B)
            gates(0)
            pe.wait_ge(attT_evac, B)
            ups(0)
            pe.wait_ge(wT_evac, KC + NC)
            pe.wait_ge(bc_evac, 2 * KC + 2)
            for i in range(T + 1):
                if i + 1 < T:
                    gates(i + 1)
                if i >= 1:
                    transpose_t(i - 1)
                    down(i - 1)
                if i + 1 < T:
                    ups(i + 1)


_INPUTS = ("x", "ctx_t", "wqk", "w_gate_up", "w_down", "down_idx_a", "down_idx_b")


def kernel(x, ctx_1024, L0_xattn_Wq, L0_xattn_bq, L0_xattn_Wk, L0_xattn_bk, L0_ffn_w_gate, L0_ffn_w_up,
           L0_ffn_w_down, L0_ffn_up_reorder_index, L0_ffn_down_reorder_index):
    import numpy as np
    import concourse.bacc as bacc
    from concourse.bass_utils import run_bass_kernel_spmd

    ctx = np.asarray(ctx_1024)
    idx = np.asarray(L0_ffn_down_reorder_index)
    full = idx.shape[0] // P * P
    arrays = {
        "x": np.ascontiguousarray(x),
        "ctx_t": np.ascontiguousarray(ctx.transpose(2, 0, 1).reshape(ctx.shape[2], -1)),
        "wqk": np.concatenate([np.asarray(L0_xattn_Wq).T, np.asarray(L0_xattn_Wk).T,
                               np.asarray(L0_xattn_bq)[:, None], np.asarray(L0_xattn_bk)[:, None]], axis=1),
        "w_gate_up": np.concatenate([np.asarray(L0_ffn_w_gate), np.asarray(L0_ffn_w_up)], axis=1),
        "w_down": np.ascontiguousarray(L0_ffn_w_down),
        "down_idx_a": np.ascontiguousarray(idx[:full].reshape(-1, P).T),
        "down_idx_b": np.ascontiguousarray(idx[full:].reshape(-1, 1)),
    }
    nc = bacc.Bacc("TRN2", target_bir_lowering=False, num_devices=1)
    aps = [nc.dram_tensor(f"{n}_dram", arrays[n].shape, mybir.dt.from_np(arrays[n].dtype),
                          kind="ExternalInput").ap() for n in _INPUTS]
    out = nc.dram_tensor("out_dram", arrays["x"].shape, F32, kind="ExternalOutput").ap()
    build(nc, *aps, out)
    r = run_bass_kernel_spmd(nc, [{f"{n}_dram": arrays[n] for n in _INPUTS}], core_ids=[0])
    return r.results[0]["out_dram"]
```

```python
from contextlib import ExitStack

import concourse.bass as bass
from concourse import mybir

P = 128
F32 = mybir.dt.float32
BF16 = mybir.dt.bfloat16
U16 = mybir.dt.uint16
I32 = mybir.dt.int32
U32 = mybir.dt.uint32
ALU = mybir.AluOpType
ACT = mybir.ActivationFunctionType
AX_X = mybir.AxisListType.X

FP8_MAX = 448.0
LN_EPS = 1e-5
GRID_SHIFT = 20
LEAST = 1.5 * 2.0 ** (GRID_SHIFT - 6)
EXPONENT_BITS = 0x7F80
HALF_BIT = 0x0040


def build(nc, x, ctx_t, wqk, w_gate_up, w_down, down_idx, out):
    B, L, N = x.shape
    C = ctx_t.shape[0]
    I = w_gate_up.shape[0]
    LT = L // P
    NC = N // P
    T = B * LT
    KC = -(-I // P)
    fresh = [min(P, I - P * k) for k in range(KC)]
    IH = I // 2
    HB = B // 2
    assert L == N and C == P and LT == 2 and NC == 2 and KC % 2 == 0

    def chunk(k):
        return slice(k * P + fresh[k] - P, k * P + fresh[k])

    with ExitStack() as ctx:
        def sb(name, shape, dt=F32):
            return ctx.enter_context(nc.sbuf_tensor(name, shape, dt))

        def bank(name, banks=1):
            return ctx.enter_context(nc.psum_tensor(name, [P, banks, 512], F32))

        def sem(name):
            return ctx.enter_context(nc.semaphore(name))

        wqk_sb = sb("wqk_sb", [P, 2 * P + 2])
        ctx_sb = sb("ctx_sb", [P, B * N])
        x_sb = sb("x_sb", [P, B, LT, N])
        idx_sb = sb("idx_sb", [P, KC], I32)
        wup_sb = sb("wup_sb", [P, KC, 2, N])
        wdn_sb = sb("wdn_sb", [P, NC, I])
        ident = sb("ident", [P, P])
        identb = sb("identb", [P, P], BF16)
        ones = sb("ones", [P, P])
        minus_half = sb("minus_half", [P, LT])
        zero = sb("zero", [P, 1])
        warm_exp = sb("warm_exp", [P, 1])
        warm_silu = sb("warm_silu", [P, 1])
        qT = sb("qT", [P, B * N])
        kT = sb("kT", [P, B * N])
        xc = sb("xc", [P, B, LT, N])
        xcT = sb("xcT", [P, B, NC, L])
        neg_max = sb("neg_max", [P, B, 2])
        att = sb("att", [P, B, 2, N])
        z = sb("z", [P, B, 2])
        rz = sb("rz", [P, B, 2])
        attT = sb("attT", [P, B, NC, N])
        bn1 = sb("bn1", [P, T, 6])
        mv1 = sb("mv1", [P, T, 2])
        ve1 = sb("ve1", [P, T])
        neg_mean1 = sb("neg_mean1", [P, T])
        rstd1 = sb("rstd1", [P, T])
        x1 = sb("x1", [P, B, LT, N])
        bn2 = sb("bn2", [P, T, 6])
        mv2 = sb("mv2", [P, T, 2])
        ve2 = sb("ve2", [P, T])
        neg_mean2 = sb("neg_mean2", [P, T])
        rstd2 = sb("rstd2", [P, T])
        xc2 = xcT
        peak_x = sb("peak_x", [P, T])
        rec_x = sb("rec_x", [P, T])
        s_x = sb("s_x", [P, T])
        s20_x = sb("s20_x", [P, T])
        rowscale = sb("rowscale", [P, T])
        grid_x = sb("grid_x", [P, B, LT, N], BF16)
        sum_x = xc
        q_x = sb("q_x", [P, B, LT, N], BF16)
        qxT = sb("qxT", [P, B, NC, L], BF16)
        peak_w = sb("peak_w", [P, KC, 2])
        rec_w = sb("rec_w", [P, KC, 2])
        s_w = sb("s_w", [P, KC, 2])
        s20_w = sb("s20_w", [P, KC, 2])
        grid_w = sb("grid_w", [P, KC, 2, N], BF16)
        sum_w = sb("sum_w", [P, KC, 2, N])
        q_w = sb("q_w", [P, KC, 2, N], BF16)
        wupT = sb("wupT", [P, NC, 2, I], BF16)
        peak_d = sb("peak_d", [P, NC])
        rec_d = sb("rec_d", [P, NC])
        s_d = sb("s_d", [P, NC])
        s20_d = sb("s20_d", [P, NC])
        grid_d = sb("grid_d", [P, NC, I], BF16)
        sum_d = sb("sum_d", [P, NC, I])
        q_d = sb("q_d", [P, NC, I], BF16)
        wdnT = sb("wdnT", [P, KC, N], BF16)
        diag = sb("diag", [P, KC + 1, 2, P])
        gate_scale = sb("gate_scale", [P, I])
        up_scale = sb("up_scale", [P, I])
        down_scale = sb("down_scale", [P, N])
        g_sb = sb("g_sb", [P, 3, I])
        act_g = sb("act_g", [P, 3, I])
        act_ws = sb("act_ws", [P, 3, I])
        t_sb = sb("t_sb", [P, 2, I])
        peak_t = sb("peak_t", [P, T])
        rec_t = sb("rec_t", [P, T])
        s_t = sb("s_t", [P, T])
        s20_t = sb("s20_t", [P, T])
        yscale = sb("yscale", [P, T])
        grid_t = sb("grid_t", [P, 2, I], BF16)
        sum_t = sb("sum_t", [P, 2, I])
        q_t = sb("q_t", [P, 2, I], BF16)
        tT = sb("tT", [P, 2, KC, P], BF16)
        y_sb = sb("y_sb", [P, 2, N])
        o_sb = sb("o_sb", [P, T, N])

        bank_a, bank_b = bank("bank_a"), bank("bank_b")
        gate_ps, up_ps = bank("gate_ps", 2), bank("up_ps", 2)
        bank_c, bank_d = bank("bank_c"), bank("bank_d")
        proj_ps = [bank_a[:, 0, :], bank_b[:, 0, :]]
        wT_ps = bank_a[:, 0, :].bitcast(BF16)
        spread_ps = bank_b[:, 0, 0:2 * P].rearrange("p (a n) -> p a n", a=2)
        scores_ps = [gate_ps[:, n, :].rearrange("p (j n) -> p j n", j=2) for n in range(2)]
        attT_ps = up_ps[:, 0, :].rearrange("p (j n) -> p j n", j=2)
        xcT_ps = up_ps[:, 1, :].rearrange("p (j n) -> p j n", j=2)
        xm_ps = bank_c[:, 0, :].rearrange("p (j n) -> p j n", j=2)
        qxT_ps = bank_d[:, 0, :].bitcast(BF16)[:, 0:NC * L].rearrange("p (j n) -> p j n", j=2)
        tT_ps = bank_b[:, 0, :].bitcast(BF16)[:, 0:KC * P].rearrange("p (k n) -> p k n", k=KC)
        y_ps = [bank_c[:, 0, 0:N], bank_a[:, 0, 0:N]]

        wqk_in = sem("wqk_in")
        ctx_in = [sem(f"ctx_in{h}") for h in range(2)]
        x_in = [sem(f"x_in{b}") for b in range(B)]
        idx_in = sem("idx_in")
        wup_in = [sem(f"wup_in{k}") for k in range(KC)]
        wdn_in = sem("wdn_in")
        out_done = sem("out_done")
        q_proj_ready = sem("q_proj_ready")
        k_proj_ready = sem("k_proj_ready")
        scores_ready = sem("scores_ready")
        xcT_ready = sem("xcT_ready")
        attT_ready = sem("attT_ready")
        xm_ready = sem("xm_ready")
        qxT_ready = sem("qxT_ready")
        wdT_ready = sem("wdT_ready")
        wuT_ready = sem("wuT_ready")
        spread_ready = sem("spread_ready")
        gate_ready = sem("gate_ready")
        up_ready = sem("up_ready")
        tT_ready = sem("tT_ready")
        y_ready = sem("y_ready")
        q_evac = sem("q_evac")
        k_evac = sem("k_evac")
        xc_done = sem("xc_done")
        exp_done = sem("exp_done")
        att_done = sem("att_done")
        xcT_evac = sem("xcT_evac")
        attT_evac = sem("attT_evac")
        xc2_done = sem("xc2_done")
        scaled_x = sem("scaled_x")
        qxT_evac = sem("qxT_evac")
        scaled_d = sem("scaled_d")
        scaled_w = sem("scaled_w")
        wdT_evac = sem("wdT_evac")
        wuT_evac = sem("wuT_evac")
        diag_done = sem("diag_done")
        spread_evac = sem("spread_evac")
        silu_done = sem("silu_done")
        scaled_t = sem("scaled_t")
        tT_evac = sem("tT_evac")
        dve_step = sem("dve_step")
        warm_ready = sem("warm_ready")
        ones_ready = sem("ones_ready")
        stats1_done = sem("stats1_done")
        max_done = sem("max_done")
        rz_done = sem("rz_done")
        x1_done = sem("x1_done")
        stats2_done = sem("stats2_done")
        peak_x_done = sem("peak_x_done")
        s_x_done = sem("s_x_done")
        sum_x_done = sem("sum_x_done")
        peak_w_done = sem("peak_w_done")
        s_w_done = sem("s_w_done")
        peak_d_done = sem("peak_d_done")
        s_d_done = sem("s_d_done")
        grid_w_done = sem("grid_w_done")
        sum_d_done = sem("sum_d_done")
        gate_scaled = sem("gate_scaled")
        t_done = sem("t_done")
        s_t_done = sem("s_t_done")
        sum_t_done = sem("sum_t_done")
        y_scaled = sem("y_scaled")
        last_q_t_done = sem("last_q_t_done")
        last_out_ready = sem("last_out_ready")
        pool_step = sem("pool_step")
        consts_ready = sem("consts_ready")
        rstd1_done = sem("rstd1_done")
        rowscale_done = sem("rowscale_done")
        q_x_done = sem("q_x_done")
        q_w_done = sem("q_w_done")
        q_d_done = sem("q_d_done")
        ws_done = sem("ws_done")
        q_t_done = sem("q_t_done")
        out_ready = sem("out_ready")

        block = ctx.enter_context(nc.Block())

        @block.sync
        def _(sp):
            def load_x(b):
                sp.dma_start(x_sb[:, b], x[b].rearrange("(j p) n -> p j n", p=P)).then_inc(x_in[b], 16)

            sp.dma_start(wqk_sb[:, :], wqk).then_inc(wqk_in, 16)
            sp.dma_start(ctx_sb[:, 0:HB * N], ctx_t[:, 0:HB * N]).then_inc(ctx_in[0], 16)
            sp.dma_start(idx_sb[:, :], down_idx).then_inc(idx_in, 16)
            load_x(0)
            load_x(1)
            sp.dma_start(ctx_sb[:, HB * N:], ctx_t[:, HB * N:]).then_inc(ctx_in[1], 16)
            sp.dma_start(wdn_sb[:, :, :], w_down.rearrange("(j p) i -> p j i", p=P)).then_inc(wdn_in, 16)
            load_x(2)
            load_x(3)
            ov = out.rearrange("b (j p) n -> (b j) p n", p=P)
            for i in range(T):
                if i < T - 1:
                    sp.wait_ge(out_ready, i + 1)
                else:
                    sp.wait_ge(last_out_ready, 1)
                sp.dma_start(ov[i], o_sb[:, i, :]).then_inc(out_done, 16)
            sp.wait_ge(out_done, 16 * T)

        @block.gpsimd
        def _(pool):
            steps = [0]
            at = {}

            def step(ins, name=None):
                ins.then_inc(pool_step, 1)
                steps[0] += 1
                at[name] = steps[0]

            def after(name):
                pool.wait_ge(pool_step, at[name])

            def gather(k):
                nc.gpsimd.indirect_dma_start(
                    out=wup_sb[:, k].rearrange("p a n -> p (a n)"), out_offset=None, in_=w_gate_up,
                    in_offset=bass.IndirectOffsetOnAxis(ap=idx_sb[:, k:k + 1], axis=0),
                ).then_inc(wup_in[k], 16)

            def rstd1_of(b):
                pair = slice(LT * b, LT * b + LT)
                pool.wait_ge(stats1_done, b + 1)
                nc.gpsimd.tensor_tensor(rstd1[:, pair], ve1[:, pair], minus_half[:, :], ALU.pow)\
                    .then_inc(rstd1_done, 1)

            def rstd2_of(b):
                pair = slice(LT * b, LT * b + LT)
                pool.wait_ge(stats2_done, b + 1)
                step(nc.gpsimd.tensor_tensor(rstd2[:, pair], ve2[:, pair], minus_half[:, :], ALU.pow), ("rstd2", b))

            def rowscale_of(b):
                pair = slice(LT * b, LT * b + LT)
                after(("rstd2", b))
                pool.wait_ge(peak_x_done, b + 1)
                nc.gpsimd.tensor_tensor(rowscale[:, pair], rstd2[:, pair], peak_x[:, pair],
                                        ALU.mult).then_inc(rowscale_done, 1)

            def subtract_x(b):
                pool.wait_ge(sum_x_done, b + 1)
                nc.gpsimd.tensor_tensor(q_x[:, b], sum_x[:, b], grid_x[:, b], ALU.subtract)\
                    .then_inc(q_x_done, 1)

            def add_grid_up(k):
                pool.wait_ge(scaled_w, 4 * k + 4)
                pool.wait_ge(grid_w_done, k + 1)
                step(nc.gpsimd.tensor_tensor(sum_w[:, k], sum_w[:, k], grid_w[:, k], ALU.add), ("sum_w", k))

            def subtract_up(k):
                after(("sum_w", k))
                nc.gpsimd.tensor_tensor(q_w[:, k], sum_w[:, k], grid_w[:, k], ALU.subtract).then_inc(q_w_done, 1)

            def subtract_down(j):
                pool.wait_ge(sum_d_done, j + 1)
                nc.gpsimd.tensor_tensor(q_d[:, j], sum_d[:, j], grid_d[:, j], ALU.subtract).then_inc(q_d_done, 1)

            def scale_act(i):
                if i == 0:
                    pool.wait_ge(spread_evac, 2 * KC + 2)
                pool.wait_ge(silu_done, i + 1)
                if i >= 3:
                    pool.wait_ge(t_done, i - 2)
                nc.gpsimd.tensor_tensor(act_ws[:, i % 3], act_g[:, i % 3], up_scale[:, :], ALU.mult)\
                    .then_inc(ws_done, 1)

            def subtract_t(i):
                pool.wait_ge(sum_t_done, i + 1)
                if i >= 2:
                    pool.wait_ge(tT_ready, i - 1)
                nc.gpsimd.tensor_tensor(q_t[:, i % 2], sum_t[:, i % 2], grid_t[:, i % 2], ALU.subtract)\
                    .then_inc(q_t_done, 1)

            def add_residual(i):
                pool.wait_ge(y_scaled, i + 1)
                nc.gpsimd.tensor_tensor(o_sb[:, i], y_sb[:, i % 2], x1[:, i // LT, i % LT], ALU.add)\
                    .then_inc(out_ready, 1)

            nc.gpsimd.memset(ident[:, :], 0.0)
            step(nc.gpsimd.memset(minus_half[:, :], -0.5), "cleared")
            after("cleared")
            step(nc.gpsimd.affine_select(out=ident[:, :], in_=ident[:, :], compare_op=ALU.not_equal, fill=1.0,
                                         base=0, pattern=[[-1, P]], channel_multiplier=1), "ident")
            after("ident")
            nc.gpsimd.tensor_copy(identb[:, :], ident[:, :]).then_inc(consts_ready, 1)
            pool.wait_ge(idx_in, 16)
            gather(0)
            gather(1)
            gather(2)
            gather(3)
            rstd1_of(0)
            gather(4)
            gather(5)
            rstd1_of(1)
            subtract_down(0)
            subtract_down(1)
            add_grid_up(0)
            add_grid_up(1)
            subtract_up(0)
            add_grid_up(2)
            subtract_up(1)
            add_grid_up(3)
            subtract_up(2)
            add_grid_up(4)
            subtract_up(3)
            subtract_up(4)
            rstd1_of(2)
            rstd2_of(0)
            add_grid_up(5)
            rowscale_of(0)
            subtract_up(5)
            subtract_x(0)
            rstd1_of(3)
            rstd2_of(1)
            rowscale_of(1)
            rstd2_of(2)
            subtract_x(1)
            scale_act(0)
            rowscale_of(2)
            scale_act(1)
            scale_act(2)
            subtract_x(2)
            rstd2_of(3)
            rowscale_of(3)
            scale_act(3)
            subtract_t(0)
            scale_act(4)
            subtract_t(1)
            scale_act(5)
            subtract_x(3)
            add_residual(0)
            subtract_t(2)
            add_residual(1)
            subtract_t(3)
            scale_act(6)
            add_residual(2)
            scale_act(7)
            subtract_t(4)
            add_residual(3)
            subtract_t(5)
            add_residual(4)
            subtract_t(6)
            add_residual(5)
            add_residual(6)

        @block.scalar
        def _(act):
            def evac_q(h):
                act.wait_ge(wqk_in, 16)
                act.wait_ge(q_proj_ready, h + 1)
                nc.scalar.activation(qT[:, h * HB * N:(h + 1) * HB * N], proj_ps[0], ACT.Identity,
                                     bias=wqk_sb[:, 2 * P:2 * P + 1]).then_inc(q_evac, 1)

            def evac_k(h):
                act.wait_ge(wqk_in, 16)
                act.wait_ge(k_proj_ready, h + 1)
                nc.scalar.activation(kT[:, h * HB * N:(h + 1) * HB * N], proj_ps[1], ACT.Identity,
                                     bias=wqk_sb[:, 2 * P + 1:2 * P + 2]).then_inc(k_evac, 1)

            def centre_x(b):
                act.wait_ge(stats1_done, b + 1)
                for j in range(LT):
                    i = LT * b + j
                    last = nc.scalar.activation(xc[:, b, j], x_sb[:, b, j], ACT.Identity,
                                                bias=neg_mean1[:, i:i + 1])
                last.then_inc(xc_done, 1)

            def exps(b):
                act.wait_ge(max_done, b + 1)
                for j in range(2):
                    last = nc.scalar.activation(att[:, b, j], scores_ps[b % 2][:, j], ACT.Exp,
                                                bias=neg_max[:, b, j:j + 1], accum_out=z[:, b, j:j + 1])
                last.then_inc(exp_done, 1)

            def normalise(b):
                act.wait_ge(exp_done, b + 1)
                act.wait_ge(rz_done, b + 1)
                for j in range(2):
                    last = nc.scalar.activation(att[:, b, j], att[:, b, j], ACT.Copy, scale=rz[:, b, j:j + 1])
                last.then_inc(att_done, 1)

            def evac_xcT(b):
                act.wait_ge(xcT_ready, b + 1)
                nc.scalar.activation(xcT[:, b], xcT_ps, ACT.Copy).then_inc(xcT_evac, 1)

            def evac_attT(b):
                act.wait_ge(attT_ready, b + 1)
                nc.scalar.activation(attT[:, b], attT_ps, ACT.Copy).then_inc(attT_evac, 1)

            def centre_x1(b):
                act.wait_ge(stats2_done, b + 1)
                for j in range(LT):
                    i = LT * b + j
                    last = nc.scalar.activation(xc2[:, b, j], x1[:, b, j], ACT.Identity,
                                                bias=neg_mean2[:, i:i + 1])
                last.then_inc(xc2_done, 1)

            def scale_x(b):
                act.wait_ge(xc2_done, b + 1)
                act.wait_ge(s_x_done, b + 1)
                for j in range(LT):
                    i = LT * b + j
                    last = nc.scalar.activation(grid_x[:, b, j], xc2[:, b, j], ACT.Copy, scale=s20_x[:, i:i + 1])
                last.then_inc(scaled_x, 1)

            def evac_qxT(b):
                act.wait_ge(qxT_ready, b + 1)
                nc.scalar.activation(qxT[:, b], qxT_ps, ACT.Copy).then_inc(qxT_evac, 1)

            def scale_down(j):
                act.wait_ge(s_d_done, j + 1)
                nc.scalar.activation(grid_d[:, j], wdn_sb[:, j], ACT.Copy, scale=s20_d[:, j:j + 1])\
                    .then_inc(scaled_d, 1)

            def scale_up(k):
                act.wait_ge(s_w_done, k + 1)
                for a in range(2):
                    nc.scalar.activation(grid_w[:, k, a], wup_sb[:, k, a], ACT.Copy,
                                         scale=s20_w[:, k, a:a + 1]).then_inc(scaled_w, 1)
                for a in range(2):
                    nc.scalar.activation(sum_w[:, k, a], wup_sb[:, k, a], ACT.Copy,
                                         scale=s_w[:, k, a:a + 1]).then_inc(scaled_w, 1)

            def evac_down(j):
                act.wait_ge(wdT_ready, j + 1)
                nc.scalar.activation(wdnT[:, :, j * P:(j + 1) * P],
                                     wT_ps[:, 0:KC * P].rearrange("p (k n) -> p k n", k=KC), ACT.Copy)\
                    .then_inc(wdT_evac, 1)

            def evac_up(k):
                act.wait_ge(wuT_ready, k + 1)
                src = wT_ps[:, 0:4 * P].rearrange("p (c a n) -> p c a n", c=2, a=2)
                nc.scalar.activation(wupT[:, :, :, k * P:k * P + fresh[k]], src[:, :, :, P - fresh[k]:], ACT.Copy)\
                    .then_inc(wuT_evac, 1)

            def diagonals(k):
                act.wait_ge(consts_ready, 1)
                if k == 0:
                    act.wait_ge(peak_d_done, NC)
                else:
                    act.wait_ge(peak_w_done, k)
                for a in range(2):
                    peak = peak_d[:, a:a + 1] if k == 0 else peak_w[:, k - 1, a:a + 1]
                    last = nc.scalar.activation(diag[:, k, a], ident[:, :], ACT.Copy, scale=peak)
                last.then_inc(diag_done, 1)

            def evac_scales(k):
                act.wait_ge(spread_ready, k + 1)
                for a in range(2):
                    if k == 0:
                        dst, src, factor = down_scale[:, a * P:(a + 1) * P], spread_ps[:, a], 1.0 / FP8_MAX
                    else:
                        r = fresh[k - 1]
                        dst = (gate_scale, up_scale)[a][:, (k - 1) * P:(k - 1) * P + r]
                        src, factor = spread_ps[:, a, P - r:], (FP8_MAX ** -2, 1.0 / FP8_MAX)[a]
                    nc.scalar.activation(dst, src, ACT.Copy, scale=factor).then_inc(spread_evac, 1)

            def load_silu():
                nc.scalar.activation(warm_silu[:, :], zero[:, :], ACT.Silu)

            def silu(i):
                act.wait_ge(gate_scaled, i + 1)
                act.wait_ge(rowscale_done, i // LT + 1)
                if i >= 3:
                    act.wait_ge(ws_done, i - 2)
                nc.scalar.activation(act_g[:, i % 3], g_sb[:, i % 3], ACT.Silu, scale=rowscale[:, i:i + 1])\
                    .then_inc(silu_done, 1)

            def scale_t(i):
                act.wait_ge(s_t_done, i + 1)
                if i >= 2:
                    act.wait_ge(q_t_done, i - 1)
                nc.scalar.activation(grid_t[:, i % 2], t_sb[:, i % 2], ACT.Copy, scale=s20_t[:, i:i + 1])\
                    .then_inc(scaled_t, 1)

            def evac_tT(i):
                act.wait_ge(tT_ready, i + 1)
                if i >= 2:
                    act.wait_ge(y_ready, i - 1)
                nc.scalar.activation(tT[:, i % 2], tT_ps, ACT.Copy).then_inc(tT_evac, 1)

            act.wait_ge(warm_ready, 1)
            nc.scalar.activation(warm_exp[:, :], zero[:, :], ACT.Exp)
            evac_q(0)
            centre_x(0)
            evac_k(0)
            centre_x(1)
            evac_xcT(0)
            evac_q(1)
            diagonals(0)
            exps(0)
            scale_down(0)
            scale_up(0)
            normalise(0)
            scale_down(1)
            scale_up(1)
            evac_attT(0)
            scale_up(2)
            exps(1)
            scale_up(3)
            evac_down(0)
            normalise(1)
            evac_k(1)
            scale_up(4)
            evac_down(1)
            centre_x1(0)
            evac_xcT(1)
            evac_attT(1)
            diagonals(1)
            evac_scales(0)
            evac_up(0)
            scale_up(5)
            diagonals(2)
            evac_scales(1)
            scale_x(0)
            evac_up(1)
            exps(2)
            diagonals(3)
            evac_scales(2)
            evac_up(2)
            centre_x(2)
            normalise(2)
            diagonals(4)
            evac_scales(3)
            evac_up(3)
            centre_x1(1)
            diagonals(5)
            evac_scales(4)
            evac_xcT(2)
            evac_attT(2)
            evac_up(4)
            exps(3)
            diagonals(6)
            evac_scales(5)
            evac_qxT(0)
            evac_up(5)
            scale_x(1)
            load_silu()
            evac_scales(6)
            centre_x(3)
            normalise(3)
            silu(0)
            centre_x1(2)
            evac_xcT(3)
            evac_attT(3)
            silu(1)
            evac_qxT(1)
            scale_x(2)
            silu(2)
            scale_t(0)
            centre_x1(3)
            evac_qxT(2)
            silu(3)
            scale_t(1)
            silu(4)
            scale_x(3)
            evac_tT(0)
            silu(5)
            scale_t(2)
            evac_tT(1)
            scale_t(3)
            evac_qxT(3)
            evac_tT(2)
            silu(6)
            scale_t(4)
            evac_tT(3)
            silu(7)
            scale_t(5)
            evac_tT(4)
            scale_t(6)
            evac_tT(5)
            scale_t(7)
            evac_tT(6)
            evac_tT(7)

        @block.vector
        def _(dve):
            steps = [0]
            at = {}

            def step(ins, name=None):
                ins.then_inc(dve_step, 1)
                steps[0] += 1
                at[name] = steps[0]

            def after(name):
                dve.wait_ge(dve_step, at[name])

            def bn_stats(which, src, bn, b):
                for j in range(LT):
                    step(nc.vector.bn_stats(bn[:, LT * b + j], src[:, b, j]), (which, "bn", b, j))

            def bn_aggr(which, bn, mv, b):
                for j in range(LT):
                    after((which, "bn", b, j))
                    step(nc.vector.bn_aggr(mv[:, LT * b + j], bn[:, LT * b + j]), (which, "mv", b))

            def finish_stats(which, mv, ve, neg_mean, done, b):
                pair = slice(LT * b, LT * b + LT)
                after((which, "mv", b))
                nc.vector.tensor_scalar(neg_mean[:, pair], mv[:, pair, 0], -1.0, None, ALU.mult)
                nc.vector.tensor_scalar(ve[:, pair], mv[:, pair, 1], LN_EPS, None, ALU.add).then_inc(done, 1)

            def bn_stats1(b):
                dve.wait_ge(x_in[b], 16)
                bn_stats(1, x_sb, bn1, b)

            def bn_aggr1(b):
                bn_aggr(1, bn1, mv1, b)

            def finish_stats1(b):
                finish_stats(1, mv1, ve1, neg_mean1, stats1_done, b)

            def bn_stats2(b):
                dve.wait_ge(x1_done, b + 1)
                bn_stats(2, x1, bn2, b)

            def bn_aggr2(b):
                bn_aggr(2, bn2, mv2, b)

            def finish_stats2(b):
                finish_stats(2, mv2, ve2, neg_mean2, stats2_done, b)

            def score_max(b):
                dve.wait_ge(scores_ready, b + 1)
                nc.vector.tensor_reduce(neg_max[:, b], scores_ps[b % 2], AX_X, ALU.max,
                                        negate=True).then_inc(max_done, 1)

            def reciprocal_of_z(b):
                dve.wait_ge(exp_done, b + 1)
                nc.vector.reciprocal(rz[:, b], z[:, b]).then_inc(rz_done, 1)

            def residual(b):
                dve.wait_ge(xm_ready, b + 1)
                dve.wait_ge(rstd1_done, b + 1)
                for j in range(LT):
                    i = LT * b + j
                    last = nc.vector.scalar_tensor_tensor(x1[:, b, j], xm_ps[:, j], rstd1[:, i:i + 1],
                                                          x_sb[:, b, j], ALU.mult, ALU.add)
                last.then_inc(x1_done, 1)

            def invert(peak, rec, name):
                step(nc.vector.reciprocal(rec, peak), ("rec", name))

            def scales(rec, s, s20, done, name):
                after(("rec", name))
                nc.vector.tensor_scalar(s, rec, FP8_MAX, None, ALU.mult)
                nc.vector.tensor_scalar(s20, rec, FP8_MAX * 2.0 ** GRID_SHIFT, None, ALU.mult).then_inc(done, 1)

            def exponents(grid, name):
                bits = grid.bitcast(U16)
                step(nc.vector.tensor_scalar(bits, bits, EXPONENT_BITS, HALF_BIT, ALU.bitwise_and,
                                             ALU.bitwise_or), ("bits", name))

            def floor(grid, name):
                after(("bits", name))
                return nc.vector.tensor_scalar(grid, grid, LEAST, None, ALU.max)

            def peak_of_x(b):
                dve.wait_ge(xc2_done, b + 1)
                nc.vector.tensor_reduce(peak_x[:, LT * b:LT * b + LT], xc2[:, b], AX_X, ALU.max,
                                        apply_absolute_value=True).then_inc(peak_x_done, 1)

            def reciprocal_x(b):
                pair = slice(LT * b, LT * b + LT)
                dve.wait_ge(peak_x_done, b + 1)
                invert(peak_x[:, pair], rec_x[:, pair], ("x", b))

            def scales_x(b):
                pair = slice(LT * b, LT * b + LT)
                scales(rec_x[:, pair], s_x[:, pair], s20_x[:, pair], s_x_done, ("x", b))

            def exponents_x(b):
                dve.wait_ge(scaled_x, b + 1)
                exponents(grid_x[:, b], ("x", b))

            def floor_x(b):
                step(floor(grid_x[:, b], ("x", b)), ("grid_x", b))

            def add_grid_x(b):
                dve.wait_ge(s_x_done, b + 1)
                after(("grid_x", b))
                for j in range(LT):
                    i = LT * b + j
                    last = nc.vector.scalar_tensor_tensor(sum_x[:, b, j], xc2[:, b, j], s_x[:, i:i + 1],
                                                          grid_x[:, b, j], ALU.mult, ALU.add)
                last.then_inc(sum_x_done, 1)

            def peak_of_up(k):
                dve.wait_ge(wup_in[k], 16)
                nc.vector.tensor_reduce(peak_w[:, k], wup_sb[:, k], AX_X, ALU.max,
                                        apply_absolute_value=True).then_inc(peak_w_done, 1)

            def reciprocal_up(k):
                dve.wait_ge(peak_w_done, k + 1)
                invert(peak_w[:, k], rec_w[:, k], ("w", k))

            def scales_up(k):
                scales(rec_w[:, k], s_w[:, k], s20_w[:, k], s_w_done, ("w", k))

            def exponents_up(k):
                dve.wait_ge(scaled_w, 4 * k + 2)
                exponents(grid_w[:, k], ("w", k))

            def floor_up(k):
                floor(grid_w[:, k], ("w", k)).then_inc(grid_w_done, 1)

            def peak_of_down(j):
                dve.wait_ge(wdn_in, 16)
                nc.vector.tensor_reduce(peak_d[:, j:j + 1], wdn_sb[:, j], AX_X, ALU.max,
                                        apply_absolute_value=True).then_inc(peak_d_done, 1)

            def reciprocal_down(j):
                dve.wait_ge(peak_d_done, j + 1)
                invert(peak_d[:, j:j + 1], rec_d[:, j:j + 1], ("d", j))

            def scales_down(j):
                scales(rec_d[:, j:j + 1], s_d[:, j:j + 1], s20_d[:, j:j + 1], s_d_done, ("d", j))

            def exponents_down(j):
                dve.wait_ge(scaled_d, j + 1)
                exponents(grid_d[:, j], ("d", j))

            def floor_down(j):
                step(floor(grid_d[:, j], ("d", j)), ("grid_d", j))

            def add_grid_down(j):
                dve.wait_ge(s_d_done, j + 1)
                after(("grid_d", j))
                nc.vector.scalar_tensor_tensor(sum_d[:, j], wdn_sb[:, j], s_d[:, j:j + 1], grid_d[:, j],
                                               ALU.mult, ALU.add).then_inc(sum_d_done, 1)

            def halves(ap):
                return ap.rearrange("p (h n) -> p h n", h=2)

            def scale_gate(i):
                if i == 0:
                    dve.wait_ge(spread_evac, 2 * KC + 2)
                dve.wait_ge(gate_ready, i + 1)
                if i >= 3:
                    dve.wait_ge(silu_done, i - 2)
                nc.vector.tensor_tensor(halves(g_sb[:, i % 3]), gate_ps[:, :, 0:IH], halves(gate_scale[:, :]),
                                        ALU.mult).then_inc(gate_scaled, 1)

            def hidden(i):
                dve.wait_ge(up_ready, i + 1)
                dve.wait_ge(ws_done, i + 1)
                if i >= 2:
                    dve.wait_ge(scaled_t, i - 1)
                    dve.wait_ge(sum_t_done, i - 1)
                nc.vector.tensor_tensor(halves(t_sb[:, i % 2]), up_ps[:, :, 0:IH], halves(act_ws[:, i % 3]),
                                        ALU.mult).then_inc(t_done, 1)

            def peak_of_t(i):
                dve.wait_ge(t_done, i + 1)
                step(nc.vector.tensor_reduce(peak_t[:, i:i + 1], t_sb[:, i % 2], AX_X, ALU.max,
                                             apply_absolute_value=True), ("peak_t", i))

            def reciprocal_t(i):
                after(("peak_t", i))
                invert(peak_t[:, i:i + 1], rec_t[:, i:i + 1], ("t", i))

            def scales_t(i):
                col = slice(i, i + 1)
                scales(rec_t[:, col], s_t[:, col], s20_t[:, col], s_t_done, ("t", i))
                dve.wait_ge(rowscale_done, i // LT + 1)
                step(nc.vector.scalar_tensor_tensor(yscale[:, col], peak_t[:, col], FP8_MAX ** -2,
                                                    rowscale[:, col], ALU.mult, ALU.mult), ("yscale", i))

            def exponents_t(i):
                dve.wait_ge(scaled_t, i + 1)
                exponents(grid_t[:, i % 2], ("t", i))

            def floor_t(i):
                step(floor(grid_t[:, i % 2], ("t", i)), ("grid_t", i))

            def add_grid_t(i):
                j, col = i % 2, slice(i, i + 1)
                dve.wait_ge(s_t_done, i + 1)
                after(("grid_t", i))
                if i >= 2:
                    dve.wait_ge(q_t_done, i - 1)
                nc.vector.scalar_tensor_tensor(sum_t[:, j], t_sb[:, j], s_t[:, col], grid_t[:, j], ALU.mult, ALU.add)\
                    .then_inc(sum_t_done, 1)

            def subtract_t(i):
                dve.wait_ge(sum_t_done, i + 1)
                dve.wait_ge(tT_ready, i - 1)
                nc.vector.tensor_tensor(q_t[:, i % 2], sum_t[:, i % 2], grid_t[:, i % 2], ALU.subtract)\
                    .then_inc(last_q_t_done, 1)

            def scale_y(i):
                dve.wait_ge(y_ready, i + 1)
                if i == 0:
                    dve.wait_ge(spread_evac, 2)
                if i >= 2:
                    dve.wait_ge(out_ready, i - 1)
                after(("yscale", i))
                nc.vector.scalar_tensor_tensor(y_sb[:, i % 2], y_ps[i % 2], yscale[:, i:i + 1], down_scale[:, :],
                                               ALU.mult, ALU.mult).then_inc(y_scaled, 1)

            def add_residual(i):
                dve.wait_ge(y_scaled, i + 1)
                nc.vector.tensor_tensor(o_sb[:, i], y_sb[:, i % 2], x1[:, i // LT, i % LT], ALU.add)\
                    .then_inc(last_out_ready, 1)

            nc.vector.memset(zero[:, :], 0.0).then_inc(warm_ready, 1)
            nc.vector.memset(ones[:, :], 1.0).then_inc(ones_ready, 1)
            bn_stats1(0)
            bn_stats1(1)
            bn_aggr1(0)
            bn_aggr1(1)
            finish_stats1(0)
            finish_stats1(1)
            peak_of_down(0)
            peak_of_down(1)
            score_max(0)
            peak_of_up(0)
            reciprocal_down(0)
            reciprocal_up(0)
            scales_down(0)
            scales_up(0)
            peak_of_up(1)
            reciprocal_of_z(0)
            reciprocal_down(1)
            reciprocal_up(1)
            scales_down(1)
            exponents_down(0)
            scales_up(1)
            floor_down(0)
            peak_of_up(2)
            add_grid_down(0)
            reciprocal_up(2)
            score_max(1)
            scales_up(2)
            peak_of_up(3)
            exponents_down(1)
            exponents_up(0)
            floor_down(1)
            reciprocal_up(3)
            add_grid_down(1)
            floor_up(0)
            scales_up(3)
            peak_of_up(4)
            exponents_up(1)
            reciprocal_up(4)
            floor_up(1)
            scales_up(4)
            exponents_up(2)
            residual(0)
            reciprocal_of_z(1)
            bn_stats2(0)
            floor_up(2)
            bn_aggr2(0)
            peak_of_up(5)
            finish_stats2(0)
            reciprocal_up(5)
            exponents_up(3)
            scales_up(5)
            floor_up(3)
            bn_stats1(2)
            bn_stats1(3)
            bn_aggr1(2)
            bn_aggr1(3)
            finish_stats1(2)
            finish_stats1(3)
            score_max(2)
            exponents_up(4)
            score_max(3)
            floor_up(4)
            peak_of_x(0)
            reciprocal_x(0)
            scales_x(0)
            residual(1)
            exponents_up(5)
            bn_stats2(1)
            floor_up(5)
            bn_aggr2(1)
            exponents_x(0)
            finish_stats2(1)
            floor_x(0)
            add_grid_x(0)
            reciprocal_of_z(2)
            peak_of_x(1)
            reciprocal_x(1)
            scales_x(1)
            reciprocal_of_z(3)
            residual(2)
            bn_stats2(2)
            exponents_x(1)
            bn_aggr2(2)
            floor_x(1)
            finish_stats2(2)
            add_grid_x(1)
            scale_gate(0)
            scale_gate(1)
            peak_of_x(2)
            reciprocal_x(2)
            scales_x(2)
            hidden(0)
            peak_of_t(0)
            residual(3)
            scale_gate(2)
            exponents_x(2)
            reciprocal_t(0)
            bn_stats2(3)
            floor_x(2)
            scales_t(0)
            hidden(1)
            add_grid_x(2)
            bn_aggr2(3)
            peak_of_t(1)
            finish_stats2(3)
            exponents_t(0)
            scale_gate(3)
            floor_t(0)
            reciprocal_t(1)
            peak_of_x(3)
            add_grid_t(0)
            scales_t(1)
            hidden(2)
            reciprocal_x(3)
            scale_gate(4)
            scales_x(3)
            exponents_t(1)
            peak_of_t(2)
            floor_t(1)
            reciprocal_t(2)
            scale_gate(5)
            add_grid_t(1)
            exponents_x(3)
            scales_t(2)
            floor_x(3)
            hidden(3)
            add_grid_x(3)
            peak_of_t(3)
            exponents_t(2)
            reciprocal_t(3)
            scale_y(0)
            floor_t(2)
            scales_t(3)
            add_grid_t(2)
            scale_y(1)
            hidden(4)
            exponents_t(3)
            peak_of_t(4)
            floor_t(3)
            scale_gate(6)
            add_grid_t(3)
            reciprocal_t(4)
            hidden(5)
            scales_t(4)
            peak_of_t(5)
            scale_gate(7)
            exponents_t(4)
            reciprocal_t(5)
            scale_y(2)
            floor_t(4)
            scales_t(5)
            add_grid_t(4)
            scale_y(3)
            hidden(6)
            exponents_t(5)
            peak_of_t(6)
            floor_t(5)
            reciprocal_t(6)
            add_grid_t(5)
            scales_t(6)
            hidden(7)
            peak_of_t(7)
            exponents_t(6)
            reciprocal_t(7)
            scale_y(4)
            floor_t(6)
            scales_t(7)
            add_grid_t(6)
            exponents_t(7)
            scale_y(5)
            floor_t(7)
            add_grid_t(7)
            subtract_t(7)
            scale_y(6)
            scale_y(7)
            add_residual(7)

        @block.tensor
        def _(pe):
            def project_q(h):
                pe.wait_ge(wqk_in, 16)
                pe.wait_ge(ctx_in[h], 16)
                if h:
                    pe.wait_ge(q_evac, h)
                nc.tensor.matmul(proj_ps[0], wqk_sb[:, 0:P], ctx_sb[:, h * HB * N:(h + 1) * HB * N],
                                 start=True, stop=True).then_inc(q_proj_ready, 1)

            def project_k(h):
                pe.wait_ge(wqk_in, 16)
                pe.wait_ge(ctx_in[h], 16)
                if h:
                    pe.wait_ge(k_evac, h)
                nc.tensor.matmul(proj_ps[1], wqk_sb[:, P:2 * P], ctx_sb[:, h * HB * N:(h + 1) * HB * N],
                                 start=True, stop=True).then_inc(k_proj_ready, 1)

            def scores(b):
                pe.wait_ge(q_evac, b // HB + 1)
                pe.wait_ge(k_evac, b // HB + 1)
                if b >= 2:
                    pe.wait_ge(exp_done, b - 1)
                for j in range(2):
                    last = nc.tensor.matmul(scores_ps[b % 2][:, j], qT[:, b * N + j * P:b * N + (j + 1) * P],
                                            kT[:, b * N:(b + 1) * N], start=True, stop=True)
                last.then_inc(scores_ready, 1)

            def transpose_xc(b):
                pe.wait_ge(consts_ready, 1)
                pe.wait_ge(xc_done, b + 1)
                if b:
                    pe.wait_ge(xcT_evac, b)
                for c in range(NC):
                    for j in range(LT):
                        last = nc.tensor.transpose(xcT_ps[:, c, j * P:(j + 1) * P], xc[:, b, j, c * P:(c + 1) * P],
                                                   ident[:, :])
                last.then_inc(xcT_ready, 1)

            def transpose_att(b):
                pe.wait_ge(consts_ready, 1)
                pe.wait_ge(att_done, b + 1)
                if b:
                    pe.wait_ge(attT_evac, b)
                for c in range(NC):
                    for j in range(2):
                        last = nc.tensor.transpose(attT_ps[:, c, j * P:(j + 1) * P], att[:, b, j, c * P:(c + 1) * P],
                                                   ident[:, :])
                last.then_inc(attT_ready, 1)

            def attend(b):
                pe.wait_ge(xcT_evac, b + 1)
                pe.wait_ge(attT_evac, b + 1)
                if b:
                    pe.wait_ge(x1_done, b)
                for j in range(LT):
                    for c in range(NC):
                        last = nc.tensor.matmul(xm_ps[:, j], xcT[:, b, c, j * P:(j + 1) * P], attT[:, b, c],
                                                start=(c == 0), stop=(c == NC - 1))
                last.then_inc(xm_ready, 1)

            def transpose_qx(b):
                pe.wait_ge(q_x_done, b + 1)
                if b:
                    pe.wait_ge(qxT_evac, b)
                for c in range(NC):
                    for j in range(LT):
                        last = nc.tensor.transpose(qxT_ps[:, c, j * P:(j + 1) * P],
                                                   q_x[:, b, j, c * P:(c + 1) * P], identb[:, :])
                last.then_inc(qxT_ready, 1)

            def transpose_down(j):
                pe.wait_ge(q_d_done, j + 1)
                if j:
                    pe.wait_ge(wdT_evac, j)
                else:
                    pe.wait_ge(q_evac, 2)
                for k in range(KC):
                    last = nc.tensor.transpose(wT_ps[:, k * P:(k + 1) * P], q_d[:, j, chunk(k)], identb[:, :])
                last.then_inc(wdT_ready, 1)

            def transpose_up(k):
                pe.wait_ge(q_w_done, k + 1)
                if k == 0:
                    pe.wait_ge(wdT_evac, NC)
                else:
                    pe.wait_ge(wuT_evac, k)
                for c in range(NC):
                    for a in range(2):
                        n = 2 * c + a
                        last = nc.tensor.transpose(wT_ps[:, n * P:(n + 1) * P], q_w[:, k, a, c * P:(c + 1) * P],
                                                   identb[:, :])
                last.then_inc(wuT_ready, 1)

            def spread(k):
                pe.wait_ge(diag_done, k + 1)
                if k == 0:
                    pe.wait_ge(ones_ready, 1)
                    pe.wait_ge(k_evac, 2)
                else:
                    pe.wait_ge(spread_evac, 2 * k)
                for a in range(2):
                    last = nc.tensor.matmul(spread_ps[:, a], ones[:, :], diag[:, k, a], start=True, stop=True)
                last.then_inc(spread_ready, 1)

            def product(i, ps, a):
                b, j = i // LT, i % LT
                for h in range(2):
                    for c in range(NC):
                        last = nc.tensor.matmul(ps[:, h, 0:IH], qxT[:, b, c, j * P:(j + 1) * P],
                                                wupT[:, c, a, h * IH:(h + 1) * IH],
                                                start=(c == 0), stop=(c == NC - 1))
                return last

            def gates(i):
                pe.wait_ge(qxT_evac, i // LT + 1)
                if i:
                    pe.wait_ge(gate_scaled, i)
                else:
                    pe.wait_ge(wuT_evac, KC)
                    pe.wait_ge(exp_done, B)
                product(i, gate_ps, 0).then_inc(gate_ready, 1)

            def ups(i):
                pe.wait_ge(qxT_evac, i // LT + 1)
                if i:
                    pe.wait_ge(t_done, i)
                else:
                    pe.wait_ge(wuT_evac, KC)
                    pe.wait_ge(attT_evac, B)
                    pe.wait_ge(xcT_evac, B)
                product(i, up_ps, 1).then_inc(up_ready, 1)

            def transpose_t(i):
                if i < T - 1:
                    pe.wait_ge(q_t_done, i + 1)
                else:
                    pe.wait_ge(last_q_t_done, 1)
                if i == 0:
                    pe.wait_ge(spread_evac, 2 * KC + 2)
                else:
                    pe.wait_ge(tT_evac, i)
                for k in range(KC):
                    last = nc.tensor.transpose(tT_ps[:, k], q_t[:, i % 2, chunk(k)], identb[:, :])
                last.then_inc(tT_ready, 1)

            def down(i):
                pe.wait_ge(tT_evac, i + 1)
                if i == 0:
                    pe.wait_ge(wdT_evac, NC)
                    pe.wait_ge(x1_done, B)
                if i == 1:
                    pe.wait_ge(wuT_evac, KC)
                if i >= 2:
                    pe.wait_ge(y_scaled, i - 1)
                for k in range(KC):
                    last = nc.tensor.matmul(y_ps[i % 2], tT[P - fresh[k]:, i % 2, k], wdnT[P - fresh[k]:, k],
                                            start=(k == 0), stop=(k == KC - 1))
                last.then_inc(y_ready, 1)

            project_q(0)
            project_k(0)
            project_q(1)
            transpose_xc(0)
            scores(0)
            scores(1)
            project_k(1)
            transpose_xc(1)
            transpose_att(0)
            transpose_down(0)
            attend(0)
            transpose_down(1)
            transpose_att(1)
            spread(0)
            scores(2)
            scores(3)
            transpose_up(0)
            attend(1)
            spread(1)
            transpose_up(1)
            spread(2)
            transpose_up(2)
            spread(3)
            transpose_up(3)
            transpose_xc(2)
            transpose_qx(0)
            transpose_att(2)
            spread(4)
            transpose_up(4)
            spread(5)
            attend(2)
            transpose_up(5)
            spread(6)
            gates(0)
            transpose_xc(3)
            gates(1)
            transpose_att(3)
            transpose_qx(1)
            ups(0)
            attend(3)
            gates(2)
            ups(1)
            gates(3)
            ups(2)
            transpose_qx(2)
            gates(4)
            ups(3)
            gates(5)
            transpose_t(0)
            down(0)
            ups(4)
            transpose_t(1)
            down(1)
            transpose_qx(3)
            gates(6)
            ups(5)
            transpose_t(2)
            gates(7)
            down(2)
            ups(6)
            transpose_t(3)
            down(3)
            ups(7)
            transpose_t(4)
            down(4)
            transpose_t(5)
            down(5)
            transpose_t(6)
            transpose_t(7)
            down(6)
            down(7)


_INPUTS = ("x", "ctx_t", "wqk", "w_gate_up", "w_down", "down_idx")


def kernel(x, ctx_1024, L0_xattn_Wq, L0_xattn_bq, L0_xattn_Wk, L0_xattn_bk, L0_ffn_w_gate, L0_ffn_w_up,
           L0_ffn_w_down, L0_ffn_up_reorder_index, L0_ffn_down_reorder_index):
    import numpy as np
    import concourse.bacc as bacc
    from concourse.bass_utils import run_bass_kernel_spmd

    ctx = np.asarray(ctx_1024)
    idx = np.asarray(L0_ffn_down_reorder_index)
    hidden = idx.shape[0]
    ends = [min(e, hidden) for e in range(P, hidden + P, P)]
    arrays = {
        "x": np.ascontiguousarray(x),
        "ctx_t": np.ascontiguousarray(ctx.transpose(2, 0, 1).reshape(ctx.shape[2], -1)),
        "wqk": np.concatenate([np.asarray(L0_xattn_Wq).T, np.asarray(L0_xattn_Wk).T,
                               np.asarray(L0_xattn_bq)[:, None], np.asarray(L0_xattn_bk)[:, None]], axis=1),
        "w_gate_up": np.concatenate([np.asarray(L0_ffn_w_gate), np.asarray(L0_ffn_w_up)], axis=1),
        "w_down": np.ascontiguousarray(L0_ffn_w_down),
        "down_idx": np.stack([idx[e - P:e] for e in ends], axis=1),
    }
    nc = bacc.Bacc("TRN2", target_bir_lowering=False, num_devices=1)
    aps = [nc.dram_tensor(f"{n}_dram", arrays[n].shape, mybir.dt.from_np(arrays[n].dtype),
                          kind="ExternalInput").ap() for n in _INPUTS]
    out = nc.dram_tensor("out_dram", arrays["x"].shape, F32, kind="ExternalOutput").ap()
    build(nc, *aps, out)
    r = run_bass_kernel_spmd(nc, [{f"{n}_dram": arrays[n] for n in _INPUTS}], core_ids=[0])
    return r.results[0]["out_dram"]
```

```python
from contextlib import ExitStack

import concourse.bass as bass
from concourse import mybir

P = 128
F32 = mybir.dt.float32
BF16 = mybir.dt.bfloat16
F32R = mybir.dt.float32r
U16 = mybir.dt.uint16
I32 = mybir.dt.int32
ALU = mybir.AluOpType
ACT = mybir.ActivationFunctionType
AX_X = mybir.AxisListType.X

FP8_MAX = 448.0
LN_EPS = 1e-5
GRID_SHIFT = 20
LEAST = 1.5 * 2.0 ** -6
EXPONENT_BITS = 0x7F80
HALF_BIT = 0x0040
WARM_UP = 6
KEEP_BUSY = 2


def build(nc, x, x_t, ctx_t, wqk, w_gate_up, w_down, down_idx, out):
    B, L, N = x.shape
    C = ctx_t.shape[0]
    I = w_gate_up.shape[0]
    LT = L // P
    NC = N // P
    T = B * LT
    KC = -(-I // P)
    fresh = [min(P, I - P * k) for k in range(KC)]
    IH = I // 2
    HB = B // 2
    POOL_ADDS = (3, 5,)
    LAST = (T - 1) % 2
    assert L == N and C == P and LT == 2 and NC == 2 and KC % 2 == 0

    def halves(ap):
        return ap.rearrange("p (h n) -> p h n", h=2)

    def part(h):
        return slice(0, KC // 2 * P) if h == 0 else slice(KC // 2 * P, I)

    def halfk(h):
        return slice(h * KC // 2, (h + 1) * KC // 2)

    def chunk(k):
        return slice(k * P + fresh[k] - P, k * P + fresh[k])

    with ExitStack() as ctx:
        def sb(name, shape, dt=F32):
            return ctx.enter_context(nc.sbuf_tensor(name, shape, dt))

        def bank(name, banks=1):
            return ctx.enter_context(nc.psum_tensor(name, [P, banks, 512], F32))

        def sem(name):
            return ctx.enter_context(nc.semaphore(name))

        wqk_sb = sb("wqk_sb", [P, 2 * P + 2])
        ctx_sb = sb("ctx_sb", [P, B * N])
        x_sb = sb("x_sb", [P, B, LT, N])
        idx_sb = sb("idx_sb", [P, KC], I32)
        wup_sb = sb("wup_sb", [P, KC, 2, N])
        wdn_sb = sb("wdn_sb", [P, NC, I])
        ident = sb("ident", [P, P])
        identb = sb("identb", [P, P], BF16)
        minus_half = sb("minus_half", [P, HB * LT])
        warm_w = sb("warm_w", [P, P])
        zero = sb("zero", [P, 1])
        warm_exp = sb("warm_exp", [P, 1])
        warm_silu = sb("warm_silu", [P, 1])
        qT = sb("qT", [P, B * N])
        kT = sb("kT", [P, B * N])
        xT = sb("xT", [P, B, NC, L])
        neg_max = sb("neg_max", [P, B, 2])
        att = sb("att", [P, B, 2, N])
        z = sb("z", [P, B, 2])
        rz = sb("rz", [P, B, 2])
        attT = sb("attT", [P, B, NC, N])
        bn1 = sb("bn1", [P, T, 6])
        mv1 = sb("mv1", [P, T, 2])
        ve1 = sb("ve1", [P, T])
        rstd1 = sb("rstd1", [P, T])
        x1 = sb("x1", [P, B, LT, N])
        bn2 = sb("bn2", [P, T, 6])
        mv2 = sb("mv2", [P, T, 2])
        ve2 = sb("ve2", [P, T])
        rstd2 = sb("rstd2", [P, T])
        xc2 = xT
        peak_x = sb("peak_x", [P, T])
        rec_x = sb("rec_x", [P, T])
        s_x = sb("s_x", [P, T])
        rowscale = sb("rowscale", [P, T])
        grid_x = sb("grid_x", [P, B, LT, N], BF16)
        sum_x = sb("sum_x", [P, B, LT, N])
        q_x = sb("q_x", [P, B, LT, N], BF16)
        qxT = sb("qxT", [P, B, NC, L])
        peak_w = sb("peak_w", [P, KC, 2])
        rec_w = sb("rec_w", [P, KC, 2])
        s_w = sb("s_w", [P, KC, 2])
        grid_w = sb("grid_w", [P, KC, 2, N], BF16)
        sum_w = sb("sum_w", [P, KC, 2, N])
        q_w = sb("q_w", [P, KC, 2, N], BF16)
        deq_w = sum_w
        w_hi = sb("w_hi", [P, NC, 2, I])
        w_lo = sb("w_lo", [P, NC, 2, I])
        peak_d = sb("peak_d", [P, NC])
        rec_d = sb("rec_d", [P, NC])
        s_d = sb("s_d", [P, NC])
        grid_d = sb("grid_d", [P, NC, I], BF16)
        sum_d = sb("sum_d", [P, NC, I])
        q_d = sb("q_d", [P, NC, I], BF16)
        wdnT = sb("wdnT", [P, KC, N], BF16)
        down_scale = sb("down_scale", [P, N])
        act_g = sb("act_g", [P, 3, I])
        t_sb = sb("t_sb", [P, 2, I])
        peak_t = sb("peak_t", [P, T])
        rec_t = sb("rec_t", [P, T])
        s_t = sb("s_t", [P, T])
        yscale = sb("yscale", [P, T])
        grid_t = sb("grid_t", [P, 2, I], BF16)
        sum_t = sb("sum_t", [P, 2, I])
        q_t = sb("q_t", [P, 2, I], BF16)
        tT = sb("tT", [P, 2, KC, P], BF16)
        y_sb = sb("y_sb", [P, 2, N])
        o_sb = sb("o_sb", [P, T, N])

        bank_a, bank_b = bank("bank_a"), bank("bank_b")
        gate_ps, up_ps = bank("gate_ps", 2), bank("up_ps", 2)
        bank_c, bank_d = bank("bank_c"), bank("bank_d")
        proj_ps = [bank_a[:, 0, :], bank_b[:, 0, :]]
        wT_ps = bank_a[:, 0, :].bitcast(BF16)
        wuT_ps = bank_a[:, 0, :].rearrange("p (c a n) -> p c a n", c=NC, a=2)
        spread_ps = bank_b[:, 0, 0:2 * P].rearrange("p (a n) -> p a n", a=2)
        scores_ps = [gate_ps[:, n, :].rearrange("p (j n) -> p j n", j=2) for n in range(2)]
        attT_ps = up_ps[:, 0, :].rearrange("p (j n) -> p j n", j=2)
        xm_ps = bank_c[:, 0, :].rearrange("p (j n) -> p j n", j=2)
        qxT_ps = bank_d[:, 0, :].bitcast(BF16)[:, 0:NC * L].rearrange("p (j n) -> p j n", j=2)
        tT_ps = bank_b[:, 0, :].bitcast(BF16)[:, 0:KC * P].rearrange("p (k n) -> p k n", k=KC)
        tT_last_ps = [tT_ps, bank_d[:, 0, :].bitcast(BF16)[:, 0:KC * P].rearrange("p (k n) -> p k n", k=KC)]
        y_ps = [bank_c[:, 0, 0:N], bank_a[:, 0, 0:N]]

        wqk_in = sem("wqk_in")
        ctx_in = [sem(f"ctx_in{h}") for h in range(2)]
        x_in = [sem(f"x_in{b}") for b in range(B)]
        xT_in = [sem(f"xT_in{h}") for h in range(2)]
        idx_in = sem("idx_in")
        wup_in = [sem(f"wup_in{k}") for k in range(KC)]
        wdn_in = sem("wdn_in")
        out_done = sem("out_done")
        q_proj_ready = sem("q_proj_ready")
        k_proj_ready = sem("k_proj_ready")
        scores_ready = sem("scores_ready")
        attT_ready = sem("attT_ready")
        xm_ready = sem("xm_ready")
        qxT_ready = sem("qxT_ready")
        wdT_ready = sem("wdT_ready")
        wuT_ready = sem("wuT_ready")
        spread_ready = sem("spread_ready")
        gate_ready = sem("gate_ready")
        up_ready = sem("up_ready")
        tT_ready = sem("tT_ready")
        tT_last_ready = sem("tT_last_ready")
        y_ready = sem("y_ready")
        q_evac = sem("q_evac")
        k_evac = sem("k_evac")
        exp_done = sem("exp_done")
        attT_evac = sem("attT_evac")
        xc2_done = sem("xc2_done")
        scaled_x = sem("scaled_x")
        qxT_evac = sem("qxT_evac")
        scaled_d = sem("scaled_d")
        scaled_w = sem("scaled_w")
        deq_done = sem("deq_done")
        w_hi_done = sem("w_hi_done")
        wdT_evac = sem("wdT_evac")
        spread_evac = sem("spread_evac")
        silu_done = sem("silu_done")
        scaled_t = sem("scaled_t")
        scaled_last = sem("scaled_last")
        tT_last_evac = sem("tT_last_evac")
        tT_evac = sem("tT_evac")
        dve_step = sem("dve_step")
        warm_ready = sem("warm_ready")
        stats1_done = sem("stats1_done")
        max_done = sem("max_done")
        rz_done = sem("rz_done")
        x1_done = sem("x1_done")
        stats2_done = sem("stats2_done")
        peak_x_done = sem("peak_x_done")
        s_x_done = sem("s_x_done")
        grid_x_done = sem("grid_x_done")
        peak_w_done = sem("peak_w_done")
        s_w_done = sem("s_w_done")
        peak_d_done = sem("peak_d_done")
        s_d_done = sem("s_d_done")
        grid_w_done = sem("grid_w_done")
        grid_d_done = sem("grid_d_done")
        w_lo_done = sem("w_lo_done")
        t_done = sem("t_done")
        peak_t_done = sem("peak_t_done")
        s_t_done = sem("s_t_done")
        grid_t_done = sem("grid_t_done")
        y_scaled = sem("y_scaled")
        sum_last_done = sem("sum_last_done")
        pool_step = sem("pool_step")
        consts_ready = sem("consts_ready")
        rstd1_done = sem("rstd1_done")
        rowscale_done = sem("rowscale_done")
        yscale_done = sem("yscale_done")
        q_x_done = sem("q_x_done")
        q_w_done = sem("q_w_done")
        q_d_done = sem("q_d_done")
        att_done = [sem(f"att_done{b}") for b in range(B)]
        sum_w_done = [sem(f"sum_w_done{k}") for k in range(KC)]
        out_ready = [sem(f"out_ready{i}") for i in range(T)]
        sum_x_done = [sem(f"sum_x_done{b}") for b in range(B)]
        sum_d_done = [sem(f"sum_d_done{j}") for j in range(NC)]
        sum_t_done = [sem(f"sum_t_done{i}") for i in range(T)]
        q_t_done = [sem(f"q_t_done{i}") for i in range(T - 1)]
        q_last_done = [sem(f"q_last_done{h}") for h in range(2)]

        block = ctx.enter_context(nc.Block())

        @block.sync
        def _(sp):
            def load_x(b):
                sp.dma_start(x_sb[:, b], x[b].rearrange("(j p) n -> p j n", p=P)).then_inc(x_in[b], 16)

            sp.dma_start(wqk_sb[:, :], wqk).then_inc(wqk_in, 16)
            sp.dma_start(ctx_sb[:, 0:HB * N], ctx_t[:, 0:HB * N]).then_inc(ctx_in[0], 16)
            load_x(3)
            sp.dma_start(idx_sb[:, :], down_idx).then_inc(idx_in, 16)
            load_x(0)
            sp.dma_start(wdn_sb[:, :, :], w_down.rearrange("(j p) i -> p j i", p=P)).then_inc(wdn_in, 16)
            load_x(2)
            sp.dma_start(ctx_sb[:, HB * N:], ctx_t[:, HB * N:]).then_inc(ctx_in[1], 16)
            load_x(1)
            sp.wait_ge(wup_in[KC - 2], 16)
            for h in range(2):
                half = slice(h * HB * NC * L, (h + 1) * HB * NC * L)
                sp.dma_start(xT[:, h * HB:(h + 1) * HB].rearrange("p b c l -> p (b c l)"), x_t[:, half])\
                    .then_inc(xT_in[h], 16)
            ov = out.rearrange("b (j p) n -> (b j) p n", p=P)
            for i in range(T):
                sp.wait_ge(out_ready[i], 1)
                sp.dma_start(ov[i], o_sb[:, i, :]).then_inc(out_done, 16)
            sp.wait_ge(out_done, 16 * T)

        @block.gpsimd
        def _(pool):
            steps = [0]
            at = {}

            def step(ins, name=None):
                ins.then_inc(pool_step, 1)
                steps[0] += 1
                at[name] = steps[0]

            def after(name):
                pool.wait_ge(pool_step, at[name])

            def gather(k):
                nc.gpsimd.indirect_dma_start(
                    out=wup_sb[:, k].rearrange("p a n -> p (a n)"), out_offset=None, in_=w_gate_up,
                    in_offset=bass.IndirectOffsetOnAxis(ap=idx_sb[:, k:k + 1], axis=0),
                ).then_inc(wup_in[k], 16)

            def add_eps1(h):
                four = slice(HB * LT * h, HB * LT * (h + 1))
                pool.wait_ge(stats1_done, HB * (h + 1))
                step(nc.gpsimd.tensor_scalar(ve1[:, four], mv1[:, four, 1], LN_EPS, 1.0, ALU.add, ALU.mult),
                     ("ve1", h))

            def rstd1_of(h):
                four = slice(HB * LT * h, HB * LT * (h + 1))
                after(("ve1", h))
                nc.gpsimd.tensor_tensor(rstd1[:, four], ve1[:, four], minus_half[:, :], ALU.pow)\
                    .then_inc(rstd1_done, 1)

            def add_eps2(h):
                four = slice(HB * LT * h, HB * LT * (h + 1))
                pool.wait_ge(stats2_done, HB * (h + 1))
                step(nc.gpsimd.tensor_scalar(ve2[:, four], mv2[:, four, 1], LN_EPS, FP8_MAX ** 4, ALU.add,
                                             ALU.mult), ("ve2", h))

            def rstd2_of(h):
                four = slice(HB * LT * h, HB * LT * (h + 1))
                after(("ve2", h))
                step(nc.gpsimd.tensor_tensor(rstd2[:, four], ve2[:, four], minus_half[:, :], ALU.pow), ("rstd2", h))

            def rowscale_of(b):
                pair = slice(LT * b, LT * b + LT)
                after(("rstd2", b // HB))
                pool.wait_ge(peak_x_done, b + 1)
                nc.gpsimd.tensor_tensor(rowscale[:, pair], rstd2[:, pair], peak_x[:, pair],
                                        ALU.mult).then_inc(rowscale_done, 1)

            def add_grid_x(b):
                pool.wait_ge(scaled_x, b + 1)
                pool.wait_ge(grid_x_done, b + 1)
                nc.gpsimd.tensor_tensor(sum_x[:, b], sum_x[:, b], grid_x[:, b], ALU.add).then_inc(sum_x_done[b], 1)

            def add_grid_down(j):
                pool.wait_ge(scaled_d, j + 1)
                pool.wait_ge(grid_d_done, j + 1)
                nc.gpsimd.tensor_tensor(sum_d[:, j], sum_d[:, j], grid_d[:, j], ALU.add).then_inc(sum_d_done[j], 1)

            def subtract_x(b):
                pool.wait_ge(sum_x_done[b], 1)
                nc.gpsimd.tensor_tensor(q_x[:, b], sum_x[:, b], grid_x[:, b], ALU.subtract)\
                    .then_inc(q_x_done, 1)

            def add_grid_up(k):
                pool.wait_ge(scaled_w, k + 1)
                pool.wait_ge(grid_w_done, k // 2 + 1)
                nc.gpsimd.tensor_tensor(sum_w[:, k], sum_w[:, k], grid_w[:, k], ALU.add).then_inc(sum_w_done[k], 1)

            def subtract_up(k):
                pool.wait_ge(sum_w_done[k], 1)
                nc.gpsimd.tensor_tensor(q_w[:, k], sum_w[:, k], grid_w[:, k], ALU.subtract).then_inc(q_w_done, 1)

            def subtract_down(j):
                pool.wait_ge(sum_d_done[j], 1)
                nc.gpsimd.tensor_tensor(q_d[:, j], sum_d[:, j], grid_d[:, j], ALU.subtract).then_inc(q_d_done, 1)

            def yscale_of(i):
                pool.wait_ge(peak_t_done, i + 1)
                pool.wait_ge(rowscale_done, i // LT + 1)
                nc.gpsimd.tensor_tensor(yscale[:, i:i + 1], rowscale[:, i:i + 1], peak_t[:, i:i + 1], ALU.mult)\
                    .then_inc(yscale_done, 1)

            def add_grid_t(i):
                pool.wait_ge(scaled_t, i + 1)
                pool.wait_ge(grid_t_done, i + 1)
                nc.gpsimd.tensor_tensor(sum_t[:, i % 2], sum_t[:, i % 2], grid_t[:, i % 2], ALU.add)\
                    .then_inc(sum_t_done[i], 1)

            def subtract_t(i):
                pool.wait_ge(sum_t_done[i], 1)
                if i >= 2:
                    pool.wait_ge(tT_ready, i - 1)
                nc.gpsimd.tensor_tensor(q_t[:, i % 2], sum_t[:, i % 2], grid_t[:, i % 2], ALU.subtract)\
                    .then_inc(q_t_done[i], 1)

            def subtract_last(h):
                pool.wait_ge(sum_last_done, h + 1)
                pool.wait_ge(tT_ready, T - 2)
                nc.gpsimd.tensor_tensor(q_t[:, LAST, part(h)], sum_t[:, LAST, part(h)], grid_t[:, LAST, part(h)],
                                        ALU.subtract).then_inc(q_last_done[h], 1)

            def add_residual(i):
                pool.wait_ge(y_scaled, i + 1)
                nc.gpsimd.tensor_tensor(o_sb[:, i], y_sb[:, i % 2], x1[:, i // LT, i % LT], ALU.add)\
                    .then_inc(out_ready[i], 1)

            nc.gpsimd.memset(ident[:, :], 0.0)
            step(nc.gpsimd.memset(minus_half[:, :], -0.5), "cleared")
            after("cleared")
            step(nc.gpsimd.affine_select(out=ident[:, :], in_=ident[:, :], compare_op=ALU.not_equal, fill=1.0,
                                         base=0, pattern=[[-1, P]], channel_multiplier=1), "ident")
            after("ident")
            nc.gpsimd.tensor_copy(identb[:, :], ident[:, :]).then_inc(consts_ready, 1)
            pool.wait_ge(idx_in, 16)
            gather(0)
            gather(1)
            gather(2)
            gather(3)
            gather(4)
            gather(5)
            add_eps1(0)
            rstd1_of(0)
            add_grid_down(0)
            subtract_down(0)
            add_grid_down(1)
            subtract_down(1)
            add_grid_up(0)
            add_grid_up(1)
            subtract_up(0)
            subtract_up(1)
            add_grid_up(2)
            add_eps1(1)
            add_grid_up(3)
            rstd1_of(1)
            subtract_up(2)
            subtract_up(3)
            subtract_up(4)
            add_grid_up(5)
            add_eps2(0)
            subtract_up(5)
            rstd2_of(0)
            rowscale_of(0)
            add_grid_x(0)
            subtract_x(0)
            rowscale_of(1)
            add_eps2(1)
            rstd2_of(1)
            rowscale_of(2)
            subtract_x(1)
            rowscale_of(3)
            yscale_of(0)
            add_grid_x(2)
            subtract_x(2)
            yscale_of(1)
            add_grid_x(3)
            subtract_t(0)
            subtract_x(3)
            yscale_of(2)
            subtract_t(1)
            yscale_of(3)
            subtract_t(2)
            add_grid_t(3)
            yscale_of(4)
            subtract_t(3)
            add_residual(0)
            yscale_of(5)
            add_residual(1)
            subtract_t(4)
            add_grid_t(5)
            yscale_of(6)
            subtract_t(5)
            yscale_of(7)
            subtract_t(6)
            subtract_last(0)
            add_residual(3)
            add_residual(4)
            add_residual(5)
            add_residual(6)

        @block.scalar
        def _(act):
            def evac_q(h):
                act.wait_ge(wqk_in, 16)
                act.wait_ge(q_proj_ready, h + 1)
                nc.scalar.activation(qT[:, h * HB * N:(h + 1) * HB * N], proj_ps[0], ACT.Identity,
                                     bias=wqk_sb[:, 2 * P:2 * P + 1]).then_inc(q_evac, 1)

            def evac_k(h):
                act.wait_ge(wqk_in, 16)
                act.wait_ge(k_proj_ready, h + 1)
                nc.scalar.activation(kT[:, h * HB * N:(h + 1) * HB * N], proj_ps[1], ACT.Identity,
                                     bias=wqk_sb[:, 2 * P + 1:2 * P + 2]).then_inc(k_evac, 1)

            def exps(b):
                act.wait_ge(max_done, b + 1)
                for j in range(2):
                    last = nc.scalar.activation(att[:, b, j], scores_ps[b % 2][:, j], ACT.Exp,
                                                bias=neg_max[:, b, j:j + 1], accum_out=z[:, b, j:j + 1])
                last.then_inc(exp_done, 1)

            def evac_attT(b):
                act.wait_ge(attT_ready, b + 1)
                nc.scalar.activation(attT[:, b], attT_ps, ACT.Copy).then_inc(attT_evac, 1)

            def centre_x1(b):
                act.wait_ge(stats2_done, b + 1)
                for j in range(LT):
                    i = LT * b + j
                    last = nc.scalar.activation(xc2[:, b, j], x1[:, b, j], ACT.Identity,
                                                bias=mv2[:, i, 0:1], scale=-1.0)
                last.then_inc(xc2_done, 1)

            def scale_x(b):
                act.wait_ge(xc2_done, b + 1)
                act.wait_ge(s_x_done, b + 1)
                for j in range(LT):
                    i = LT * b + j
                    last = nc.scalar.activation(sum_x[:, b, j], xc2[:, b, j], ACT.Copy, scale=s_x[:, i:i + 1])
                last.then_inc(scaled_x, 1)

            def evac_qxT(b):
                act.wait_ge(qxT_ready, b + 1)
                nc.scalar.activation(qxT[:, b].bitcast(F32R), qxT_ps, ACT.Copy, scale=-1.0).then_inc(qxT_evac, 1)

            def scale_down(j):
                act.wait_ge(s_d_done, 1)
                nc.scalar.activation(sum_d[:, j], wdn_sb[:, j], ACT.Copy, scale=s_d[:, j:j + 1])\
                    .then_inc(scaled_d, 1)

            def scale_up(k):
                act.wait_ge(s_w_done, k // 2 + 1)
                for a in range(2):
                    last = nc.scalar.activation(sum_w[:, k, a], wup_sb[:, k, a], ACT.Copy, scale=s_w[:, k, a:a + 1])
                last.then_inc(scaled_w, 1)

            def evac_down(j):
                act.wait_ge(wdT_ready, j + 1)
                nc.scalar.activation(wdnT[:, :, j * P:(j + 1) * P],
                                     wT_ps[:, 0:KC * P].rearrange("p (k n) -> p k n", k=KC), ACT.Copy)\
                    .then_inc(wdT_evac, 1)

            def dequantise(k):
                act.wait_ge(q_w_done, k + 1)
                act.wait_ge(peak_w_done, k // 2 + 1)
                for a in range(2):
                    last = nc.scalar.activation(deq_w[:, k, a], q_w[:, k, a], ACT.Copy, scale=peak_w[:, k, a:a + 1])
                last.then_inc(deq_done, 1)

            def evac_up(k):
                act.wait_ge(wuT_ready, k + 1)
                cols = slice(k * P, k * P + fresh[k])
                nc.scalar.activation(w_hi[:, :, :, cols].bitcast(F32R), wuT_ps[:, :, :, P - fresh[k]:], ACT.Copy)\
                    .then_inc(w_hi_done, 1)

            def evac_scales():
                act.wait_ge(spread_ready, 1)
                nc.scalar.activation(down_scale[:, :].rearrange("p (a n) -> p a n", a=2), spread_ps, ACT.Copy,
                                     scale=FP8_MAX ** -2).then_inc(spread_evac, 1)

            def load_silu():
                nc.scalar.activation(warm_silu[:, :], zero[:, :], ACT.Silu)

            def silu(i):
                act.wait_ge(gate_ready, i + 1)
                act.wait_ge(rowscale_done, i // LT + 1)
                if i >= 3:
                    act.wait_ge(t_done, i - 2)
                nc.scalar.activation(halves(act_g[:, i % 3]), gate_ps[:, :, 0:IH], ACT.Silu,
                                     scale=rowscale[:, i:i + 1]).then_inc(silu_done, 1)

            def scale_t(i):
                act.wait_ge(s_t_done, i + 1)
                if i >= 2:
                    act.wait_ge(q_t_done[i - 2], 1)
                dst = sum_t if i in POOL_ADDS else grid_t
                nc.scalar.activation(dst[:, i % 2], t_sb[:, i % 2], ACT.Copy, scale=s_t[:, i:i + 1])\
                    .then_inc(scaled_t, 1)

            def evac_tT(i):
                act.wait_ge(tT_ready, i + 1)
                if i >= 2:
                    act.wait_ge(y_ready, i - 1)
                nc.scalar.activation(tT[:, i % 2], tT_ps, ACT.Copy).then_inc(tT_evac, 1)

            def scale_last(h):
                act.wait_ge(s_t_done, T)
                act.wait_ge(q_t_done[T - 3], 1)
                nc.scalar.activation(grid_t[:, LAST, part(h)], t_sb[:, LAST, part(h)], ACT.Copy,
                                     scale=s_t[:, T - 1:T]).then_inc(scaled_last, 1)

            def evac_last(h):
                act.wait_ge(tT_last_ready, h + 1)
                act.wait_ge(y_ready, T - 2)
                nc.scalar.activation(tT[:, LAST, halfk(h)], tT_last_ps[h][:, halfk(h)], ACT.Copy)\
                    .then_inc(tT_last_evac, 1)

            act.wait_ge(warm_ready, 1)
            nc.scalar.activation(warm_exp[:, :], zero[:, :], ACT.Exp)
            evac_k(0)
            evac_q(0)
            scale_down(0)
            scale_down(1)
            evac_k(1)
            scale_up(0)
            scale_up(1)
            evac_scales()
            exps(0)
            scale_up(2)
            evac_q(1)
            scale_up(3)
            exps(1)
            evac_down(0)
            evac_attT(0)
            scale_up(4)
            scale_up(5)
            evac_down(1)
            evac_attT(1)
            dequantise(0)
            dequantise(1)
            exps(2)
            evac_up(0)
            exps(3)
            centre_x1(0)
            evac_up(1)
            dequantise(2)
            evac_attT(2)
            dequantise(3)
            evac_up(2)
            dequantise(4)
            scale_x(0)
            evac_up(3)
            dequantise(5)
            evac_attT(3)
            centre_x1(1)
            evac_up(4)
            load_silu()
            evac_qxT(0)
            evac_up(5)
            scale_x(1)
            centre_x1(2)
            centre_x1(3)
            silu(0)
            scale_x(2)
            silu(1)
            evac_qxT(1)
            scale_x(3)
            scale_t(0)
            silu(2)
            scale_t(1)
            silu(3)
            evac_qxT(2)
            evac_tT(0)
            scale_t(2)
            silu(4)
            scale_t(3)
            evac_tT(1)
            evac_qxT(3)
            silu(5)
            scale_t(4)
            silu(6)
            evac_tT(2)
            scale_t(5)
            silu(7)
            evac_tT(3)
            scale_t(6)
            evac_tT(4)
            scale_last(0)
            scale_last(1)
            evac_tT(5)
            evac_tT(6)
            evac_last(0)
            evac_last(1)

        @block.vector
        def _(dve):
            steps = [0]
            at = {}

            def step(ins, name=None):
                ins.then_inc(dve_step, 1)
                steps[0] += 1
                at[name] = steps[0]

            def after(name):
                dve.wait_ge(dve_step, at[name])

            def bn_stats(which, src, bn, b):
                for j in range(LT):
                    step(nc.vector.bn_stats(bn[:, LT * b + j], src[:, b, j]), (which, "bn", b, j))

            def bn_aggr(which, bn, mv, done, b):
                for j in range(LT):
                    after((which, "bn", b, j))
                    last = nc.vector.bn_aggr(mv[:, LT * b + j], bn[:, LT * b + j])
                last.then_inc(done, 1)

            def bn_stats1(b):
                dve.wait_ge(x_in[b], 16)
                bn_stats(1, x_sb, bn1, b)

            def bn_aggr1(b):
                bn_aggr(1, bn1, mv1, stats1_done, b)

            def bn_stats2(b):
                dve.wait_ge(x1_done, b + 1)
                bn_stats(2, x1, bn2, b)

            def bn_aggr2(b):
                bn_aggr(2, bn2, mv2, stats2_done, b)

            def score_max(b):
                dve.wait_ge(scores_ready, b + 1)
                nc.vector.tensor_reduce(neg_max[:, b], scores_ps[b % 2], AX_X, ALU.max,
                                        negate=True).then_inc(max_done, 1)

            def reciprocal_of_z(b):
                dve.wait_ge(exp_done, b + 1)
                nc.vector.reciprocal(rz[:, b], z[:, b]).then_inc(rz_done, 1)

            def normalise(b):
                dve.wait_ge(rz_done, b + 1)
                for j in range(2):
                    last = nc.vector.tensor_scalar(att[:, b, j], att[:, b, j], rz[:, b, j:j + 1], 1.0 / N,
                                                   ALU.mult, ALU.subtract)
                last.then_inc(att_done[b], 1)

            def residual(b):
                dve.wait_ge(xm_ready, b + 1)
                dve.wait_ge(rstd1_done, b // HB + 1)
                for j in range(LT):
                    i = LT * b + j
                    last = nc.vector.scalar_tensor_tensor(x1[:, b, j], xm_ps[:, j], rstd1[:, i:i + 1],
                                                          x_sb[:, b, j], ALU.mult, ALU.add)
                last.then_inc(x1_done, 1)

            def invert(peak, rec, name):
                step(nc.vector.reciprocal(rec, peak), ("rec", name))

            def scales(rec, s, done, name):
                after(("rec", name))
                nc.vector.tensor_scalar(s, rec, FP8_MAX, None, ALU.mult).then_inc(done, 1)

            def exponents(grid, v_bits, name):
                step(nc.vector.tensor_scalar(grid.bitcast(U16), v_bits, EXPONENT_BITS, HALF_BIT, ALU.bitwise_and,
                                             ALU.bitwise_or), ("bits", name))

            def floor(grid, name):
                after(("bits", name))
                return nc.vector.tensor_scalar(grid, grid, LEAST, 2.0 ** GRID_SHIFT, ALU.max, ALU.mult)

            def peak_of_x(b):
                dve.wait_ge(xc2_done, b + 1)
                nc.vector.tensor_reduce(peak_x[:, LT * b:LT * b + LT], xc2[:, b], AX_X, ALU.max,
                                        apply_absolute_value=True).then_inc(peak_x_done, 1)

            def reciprocal_x(b):
                pair = slice(LT * b, LT * b + LT)
                dve.wait_ge(peak_x_done, b + 1)
                invert(peak_x[:, pair], rec_x[:, pair], ("x", b))

            def scales_x(b):
                pair = slice(LT * b, LT * b + LT)
                scales(rec_x[:, pair], s_x[:, pair], s_x_done, ("x", b))

            def upper_halves(v):
                return v.bitcast(U16).rearrange("p (n u) -> p n u", u=2)[:, :, 1]

            def exponents_x(b):
                dve.wait_ge(scaled_x, b + 1)
                exponents(grid_x[:, b].rearrange("p j n -> p (j n)"),
                          upper_halves(sum_x[:, b].rearrange("p j n -> p (j n)")), ("x", b))

            def floor_x(b):
                floor(grid_x[:, b], ("x", b)).then_inc(grid_x_done, 1)

            def add_grid_x(b):
                dve.wait_ge(scaled_x, b + 1)
                dve.wait_ge(grid_x_done, b + 1)
                nc.vector.tensor_tensor(sum_x[:, b], sum_x[:, b], grid_x[:, b], ALU.add).then_inc(sum_x_done[b], 1)

            def peak_of_up(p):
                pair = slice(2 * p, 2 * p + 2)
                dve.wait_ge(wup_in[2 * p], 16)
                dve.wait_ge(wup_in[2 * p + 1], 16)
                nc.vector.tensor_reduce(peak_w[:, pair], wup_sb[:, pair], AX_X, ALU.max,
                                        apply_absolute_value=True).then_inc(peak_w_done, 1)

            def reciprocal_up(p):
                pair = slice(2 * p, 2 * p + 2)
                dve.wait_ge(peak_w_done, p + 1)
                invert(peak_w[:, pair], rec_w[:, pair], ("w", p))

            def scales_up(p):
                pair = slice(2 * p, 2 * p + 2)
                scales(rec_w[:, pair], s_w[:, pair], s_w_done, ("w", p))

            def exponents_up(p):
                pair = slice(2 * p, 2 * p + 2)
                dve.wait_ge(scaled_w, 2 * p + 2)
                exponents(grid_w[:, pair].rearrange("p k a n -> p (k a n)"),
                          upper_halves(sum_w[:, pair].rearrange("p k a n -> p (k a n)")), ("w", p))

            def floor_up(p):
                floor(grid_w[:, 2 * p:2 * p + 2], ("w", p)).then_inc(grid_w_done, 1)

            def add_grid_up(k):
                dve.wait_ge(scaled_w, k + 1)
                dve.wait_ge(grid_w_done, k // 2 + 1)
                nc.vector.tensor_tensor(sum_w[:, k], sum_w[:, k], grid_w[:, k], ALU.add).then_inc(sum_w_done[k], 1)

            def peak_of_down():
                dve.wait_ge(wdn_in, 16)
                nc.vector.tensor_reduce(peak_d[:, :], wdn_sb[:, :, :], AX_X, ALU.max,
                                        apply_absolute_value=True).then_inc(peak_d_done, 1)

            def reciprocal_down():
                dve.wait_ge(peak_d_done, 1)
                invert(peak_d[:, :], rec_d[:, :], "d")

            def scales_down():
                scales(rec_d[:, :], s_d[:, :], s_d_done, "d")

            def exponents_down(j):
                dve.wait_ge(scaled_d, j + 1)
                exponents(grid_d[:, j], upper_halves(sum_d[:, j]), ("d", j))

            def floor_down(j):
                floor(grid_d[:, j], ("d", j)).then_inc(grid_d_done, 1)

            def split_up(k):
                dve.wait_ge(w_hi_done, k + 1)
                cols = slice(k * P, k * P + fresh[k])
                nc.vector.tensor_tensor(w_lo[:, :, :, cols].bitcast(F32R), wuT_ps[:, :, :, P - fresh[k]:],
                                        w_hi[:, :, :, cols], ALU.subtract).then_inc(w_lo_done, 1)

            def hidden(i):
                dve.wait_ge(up_ready, i + 1)
                dve.wait_ge(silu_done, i + 1)
                if i >= 2:
                    dve.wait_ge(scaled_t, i - 1)
                    dve.wait_ge(sum_t_done[i - 2], 1)
                nc.vector.tensor_tensor(halves(t_sb[:, i % 2]), up_ps[:, :, 0:IH], halves(act_g[:, i % 3]),
                                        ALU.mult).then_inc(t_done, 1)

            def peak_of_t(i):
                dve.wait_ge(t_done, i + 1)
                nc.vector.tensor_reduce(peak_t[:, i:i + 1], t_sb[:, i % 2], AX_X, ALU.max,
                                        apply_absolute_value=True).then_inc(peak_t_done, 1)

            def reciprocal_t(i):
                dve.wait_ge(peak_t_done, i + 1)
                invert(peak_t[:, i:i + 1], rec_t[:, i:i + 1], ("t", i))

            def scales_t(i):
                col = slice(i, i + 1)
                scales(rec_t[:, col], s_t[:, col], s_t_done, ("t", i))

            def exponents_t(i):
                dve.wait_ge(scaled_t, i + 1)
                grid = grid_t[:, i % 2]
                if i in POOL_ADDS:
                    if i >= 2:
                        dve.wait_ge(q_t_done[i - 2], 1)
                    exponents(grid, upper_halves(sum_t[:, i % 2]), ("t", i))
                else:
                    exponents(grid, grid.bitcast(U16), ("t", i))

            def floor_t(i):
                floor(grid_t[:, i % 2], ("t", i)).then_inc(grid_t_done, 1)

            def add_grid_t(i):
                j, col = i % 2, slice(i, i + 1)
                dve.wait_ge(s_t_done, i + 1)
                dve.wait_ge(grid_t_done, i + 1)
                if i >= 2:
                    dve.wait_ge(q_t_done[i - 2], 1)
                nc.vector.scalar_tensor_tensor(sum_t[:, j], t_sb[:, j], s_t[:, col], grid_t[:, j], ALU.mult, ALU.add)\
                    .then_inc(sum_t_done[i], 1)

            def exponents_last(h):
                dve.wait_ge(scaled_last, h + 1)
                grid = grid_t[:, LAST, part(h)]
                exponents(grid, grid.bitcast(U16), ("last", h))

            def floor_last(h):
                step(floor(grid_t[:, LAST, part(h)], ("last", h)), ("grid_last", h))

            def add_grid_last(h):
                dve.wait_ge(s_t_done, T)
                after(("grid_last", h))
                nc.vector.scalar_tensor_tensor(sum_t[:, LAST, part(h)], t_sb[:, LAST, part(h)], s_t[:, T - 1:T],
                                               grid_t[:, LAST, part(h)], ALU.mult, ALU.add)\
                    .then_inc(sum_last_done, 1)

            def subtract_last(h):
                dve.wait_ge(sum_last_done, h + 1)
                dve.wait_ge(tT_ready, T - 2)
                nc.vector.tensor_tensor(q_t[:, LAST, part(h)], sum_t[:, LAST, part(h)], grid_t[:, LAST, part(h)],
                                        ALU.subtract).then_inc(q_last_done[h], 1)

            def scale_y(i):
                dve.wait_ge(y_ready, i + 1)
                if i == 0:
                    dve.wait_ge(spread_evac, 1)
                if i >= 2:
                    dve.wait_ge(out_ready[i - 2], 1)
                dve.wait_ge(yscale_done, i + 1)
                nc.vector.scalar_tensor_tensor(y_sb[:, i % 2], y_ps[i % 2], yscale[:, i:i + 1], down_scale[:, :],
                                               ALU.mult, ALU.mult).then_inc(y_scaled, 1)

            def add_residual(i):
                dve.wait_ge(y_scaled, i + 1)
                nc.vector.tensor_tensor(o_sb[:, i], y_sb[:, i % 2], x1[:, i // LT, i % LT], ALU.add)\
                    .then_inc(out_ready[i], 1)

            nc.vector.memset(zero[:, :], 0.0).then_inc(warm_ready, 1)
            nc.vector.memset(warm_w[:, :], 0.0).then_inc(warm_ready, 1)
            bn_stats1(0)
            bn_aggr1(0)
            peak_of_down()
            reciprocal_down()
            scales_down()
            bn_stats1(1)
            bn_stats1(2)
            bn_aggr1(1)
            exponents_down(0)
            peak_of_up(0)
            floor_down(0)
            reciprocal_up(0)
            bn_aggr1(2)
            scales_up(0)
            peak_of_up(1)
            score_max(0)
            reciprocal_up(1)
            exponents_down(1)
            scales_up(1)
            floor_down(1)
            exponents_up(0)
            reciprocal_of_z(0)
            score_max(1)
            normalise(0)
            floor_up(0)
            peak_of_up(2)
            exponents_up(1)
            reciprocal_up(2)
            reciprocal_of_z(1)
            scales_up(2)
            normalise(1)
            floor_up(1)
            bn_stats1(3)
            score_max(2)
            exponents_up(2)
            score_max(3)
            floor_up(2)
            bn_aggr1(3)
            add_grid_up(4)
            residual(0)
            bn_stats2(0)
            reciprocal_of_z(2)
            bn_aggr2(0)
            split_up(0)
            normalise(2)
            reciprocal_of_z(3)
            residual(1)
            peak_of_x(0)
            split_up(1)
            normalise(3)
            bn_stats2(1)
            reciprocal_x(0)
            bn_aggr2(1)
            scales_x(0)
            split_up(2)
            residual(2)
            exponents_x(0)
            split_up(3)
            floor_x(0)
            bn_stats2(2)
            bn_aggr2(2)
            peak_of_x(1)
            split_up(4)
            reciprocal_x(1)
            residual(3)
            scales_x(1)
            bn_stats2(3)
            split_up(5)
            bn_aggr2(3)
            exponents_x(1)
            floor_x(1)
            peak_of_x(2)
            add_grid_x(1)
            reciprocal_x(2)
            peak_of_x(3)
            scales_x(2)
            hidden(0)
            reciprocal_x(3)
            peak_of_t(0)
            exponents_x(2)
            reciprocal_t(0)
            scales_x(3)
            floor_x(2)
            scales_t(0)
            hidden(1)
            exponents_x(3)
            peak_of_t(1)
            exponents_t(0)
            reciprocal_t(1)
            floor_t(0)
            scales_t(1)
            floor_x(3)
            add_grid_t(0)
            exponents_t(1)
            hidden(2)
            floor_t(1)
            peak_of_t(2)
            add_grid_t(1)
            reciprocal_t(2)
            hidden(3)
            scales_t(2)
            peak_of_t(3)
            reciprocal_t(3)
            exponents_t(2)
            scales_t(3)
            floor_t(2)
            add_grid_t(2)
            exponents_t(3)
            hidden(4)
            floor_t(3)
            peak_of_t(4)
            scale_y(0)
            reciprocal_t(4)
            scale_y(1)
            scales_t(4)
            hidden(5)
            peak_of_t(5)
            exponents_t(4)
            reciprocal_t(5)
            floor_t(4)
            scales_t(5)
            add_grid_t(4)
            exponents_t(5)
            hidden(6)
            floor_t(5)
            peak_of_t(6)
            scale_y(2)
            reciprocal_t(6)
            add_residual(2)
            scales_t(6)
            hidden(7)
            peak_of_t(7)
            exponents_t(6)
            reciprocal_t(7)
            floor_t(6)
            scales_t(7)
            add_grid_t(6)
            exponents_last(0)
            exponents_last(1)
            floor_last(0)
            floor_last(1)
            add_grid_last(0)
            add_grid_last(1)
            scale_y(3)
            scale_y(4)
            subtract_last(1)
            scale_y(5)
            scale_y(6)
            scale_y(7)
            add_residual(7)

        @block.tensor
        def _(pe):
            def project_q(h):
                pe.wait_ge(wqk_in, 16)
                pe.wait_ge(ctx_in[h], 16)
                if h:
                    pe.wait_ge(q_evac, h)
                nc.tensor.matmul(proj_ps[0], wqk_sb[:, 0:P], ctx_sb[:, h * HB * N:(h + 1) * HB * N],
                                 start=True, stop=True).then_inc(q_proj_ready, 1)

            def project_k(h):
                pe.wait_ge(wqk_in, 16)
                pe.wait_ge(ctx_in[h], 16)
                if h:
                    pe.wait_ge(k_evac, h)
                nc.tensor.matmul(proj_ps[1], wqk_sb[:, P:2 * P], ctx_sb[:, h * HB * N:(h + 1) * HB * N],
                                 start=True, stop=True).then_inc(k_proj_ready, 1)

            def scores(b):
                pe.wait_ge(q_evac, b // HB + 1)
                pe.wait_ge(k_evac, b // HB + 1)
                if b >= 2:
                    pe.wait_ge(exp_done, b - 1)
                for j in range(2):
                    last = nc.tensor.matmul(scores_ps[b % 2][:, j], qT[:, b * N + j * P:b * N + (j + 1) * P],
                                            kT[:, b * N:(b + 1) * N], start=True, stop=True)
                last.then_inc(scores_ready, 1)

            def transpose_att(b):
                pe.wait_ge(consts_ready, 1)
                pe.wait_ge(att_done[b], 1)
                if b:
                    pe.wait_ge(attT_evac, b)
                for c in range(NC):
                    for j in range(2):
                        last = nc.tensor.transpose(attT_ps[:, c, j * P:(j + 1) * P], att[:, b, j, c * P:(c + 1) * P],
                                                   ident[:, :])
                last.then_inc(attT_ready, 1)

            def attend(b):
                pe.wait_ge(xT_in[b // HB], 16)
                pe.wait_ge(attT_evac, b + 1)
                if b:
                    pe.wait_ge(x1_done, b)
                for j in range(LT):
                    for c in range(NC):
                        last = nc.tensor.matmul(xm_ps[:, j], xT[:, b, c, j * P:(j + 1) * P], attT[:, b, c],
                                                start=(c == 0), stop=(c == NC - 1))
                last.then_inc(xm_ready, 1)

            def transpose_qx(b):
                pe.wait_ge(q_x_done, b + 1)
                if b:
                    pe.wait_ge(qxT_evac, b)
                for c in range(NC):
                    for j in range(LT):
                        last = nc.tensor.transpose(qxT_ps[:, c, j * P:(j + 1) * P],
                                                   q_x[:, b, j, c * P:(c + 1) * P], identb[:, :])
                last.then_inc(qxT_ready, 1)

            def transpose_down(j):
                pe.wait_ge(q_d_done, j + 1)
                if j:
                    pe.wait_ge(wdT_evac, j)
                else:
                    pe.wait_ge(q_evac, 2)
                for k in range(KC):
                    last = nc.tensor.transpose(wT_ps[:, k * P:(k + 1) * P], q_d[:, j, chunk(k)], identb[:, :])
                last.then_inc(wdT_ready, 1)

            def transpose_up(k):
                pe.wait_ge(deq_done, k + 1)
                if k == 0:
                    pe.wait_ge(wdT_evac, NC)
                else:
                    pe.wait_ge(w_lo_done, k)
                for c in range(NC):
                    for a in range(2):
                        last = nc.tensor.transpose(wuT_ps[:, c, a], deq_w[:, k, a, c * P:(c + 1) * P], ident[:, :])
                last.then_inc(wuT_ready, 1)

            def spread():
                pe.wait_ge(consts_ready, 1)
                pe.wait_ge(peak_d_done, 1)
                pe.wait_ge(k_evac, 2)
                for a in range(2):
                    last = nc.tensor.matmul(spread_ps[:, a], peak_d[:, a:a + 1].to_broadcast([P, P]), ident[:, :],
                                            start=True, stop=True)
                last.then_inc(spread_ready, 1)

            def product(i, ps, a):
                b, j = i // LT, i % LT
                for h in range(2):
                    for c in range(NC):
                        for w in (w_hi, w_lo):
                            last = nc.tensor.matmul(ps[:, h, 0:IH], qxT[:, b, c, j * P:(j + 1) * P].bitcast(F32R),
                                                    w[:, c, a, h * IH:(h + 1) * IH].bitcast(F32R),
                                                    start=(c == 0 and w is w_hi), stop=(c == NC - 1 and w is w_lo))
                return last

            def gates(i):
                pe.wait_ge(qxT_evac, i // LT + 1)
                if i:
                    pe.wait_ge(silu_done, i)
                else:
                    pe.wait_ge(w_lo_done, KC)
                    pe.wait_ge(exp_done, B)
                product(i, gate_ps, 0).then_inc(gate_ready, 1)

            def ups(i):
                pe.wait_ge(qxT_evac, i // LT + 1)
                if i:
                    pe.wait_ge(t_done, i)
                else:
                    pe.wait_ge(w_lo_done, KC)
                    pe.wait_ge(attT_evac, B)
                product(i, up_ps, 1).then_inc(up_ready, 1)

            def transpose_t(i):
                pe.wait_ge(q_t_done[i], 1)
                if i == 0:
                    pe.wait_ge(spread_evac, 1)
                else:
                    pe.wait_ge(tT_evac, i)
                for k in range(KC):
                    last = nc.tensor.transpose(tT_ps[:, k], q_t[:, i % 2, chunk(k)], identb[:, :])
                last.then_inc(tT_ready, 1)

            def down(i):
                pe.wait_ge(tT_evac, i + 1)
                if i == 0:
                    pe.wait_ge(wdT_evac, NC)
                    pe.wait_ge(x1_done, B)
                if i == 1:
                    pe.wait_ge(w_lo_done, KC)
                if i >= 2:
                    pe.wait_ge(y_scaled, i - 1)
                for k in range(KC):
                    last = nc.tensor.matmul(y_ps[i % 2], tT[P - fresh[k]:, i % 2, k], wdnT[P - fresh[k]:, k],
                                            start=(k == 0), stop=(k == KC - 1))
                last.then_inc(y_ready, 1)

            def transpose_last(h):
                pe.wait_ge(q_last_done[h], 1)
                if h == 0:
                    pe.wait_ge(tT_evac, T - 1)
                else:
                    pe.wait_ge(qxT_evac, B)
                for k in range(h * KC // 2, (h + 1) * KC // 2):
                    last = nc.tensor.transpose(tT_last_ps[h][:, k], q_t[:, LAST, chunk(k)], identb[:, :])
                last.then_inc(tT_last_ready, 1)

            def down_last(h):
                pe.wait_ge(tT_last_evac, h + 1)
                pe.wait_ge(y_scaled, T - 2)
                for k in range(h * KC // 2, (h + 1) * KC // 2):
                    last = nc.tensor.matmul(y_ps[LAST], tT[P - fresh[k]:, LAST, k], wdnT[P - fresh[k]:, k],
                                            start=(k == 0), stop=(k == KC - 1))
                if h == 1:
                    last.then_inc(y_ready, 1)

            def keep_busy(n):
                if n == 0:
                    pe.wait_ge(silu_done, T)
                for _ in range(KEEP_BUSY):
                    nc.tensor.matmul(gate_ps[:, 0, 0:P], warm_w[:, :], warm_w[:, :], start=True, stop=True)

            pe.wait_ge(warm_ready, 2)
            for _ in range(WARM_UP):
                nc.tensor.matmul(scores_ps[0][:, 0, 0:P], warm_w[:, :], warm_w[:, :], start=True, stop=True)
            project_k(0)
            project_q(0)
            scores(0)
            project_k(1)
            scores(1)
            spread()
            project_q(1)
            transpose_down(0)
            transpose_att(0)
            scores(2)
            transpose_att(1)
            transpose_down(1)
            scores(3)
            attend(0)
            transpose_up(0)
            attend(1)
            transpose_up(1)
            transpose_att(2)
            transpose_up(2)
            attend(2)
            transpose_up(3)
            transpose_att(3)
            transpose_up(4)
            attend(3)
            transpose_qx(0)
            transpose_up(5)
            gates(0)
            ups(0)
            gates(1)
            transpose_qx(1)
            ups(1)
            gates(2)
            ups(2)
            gates(3)
            transpose_qx(2)
            ups(3)
            transpose_t(0)
            gates(4)
            transpose_qx(3)
            ups(4)
            transpose_t(1)
            down(0)
            gates(5)
            down(1)
            ups(5)
            gates(6)
            transpose_t(2)
            ups(6)
            gates(7)
            transpose_t(3)
            down(2)
            keep_busy(0)
            ups(7)
            transpose_t(4)
            keep_busy(1)
            keep_busy(2)
            keep_busy(3)
            keep_busy(4)
            transpose_t(5)
            keep_busy(5)
            keep_busy(6)
            keep_busy(7)
            down(3)
            down(4)
            transpose_t(6)
            down(5)
            transpose_last(0)
            transpose_last(1)
            down(6)
            down_last(0)
            down_last(1)


_INPUTS = ("x", "x_t", "ctx_t", "wqk", "w_gate_up", "w_down", "down_idx")


def kernel(x, ctx_1024, L0_xattn_Wq, L0_xattn_bq, L0_xattn_Wk, L0_xattn_bk, L0_ffn_w_gate, L0_ffn_w_up,
           L0_ffn_w_down, L0_ffn_up_reorder_index, L0_ffn_down_reorder_index):
    import numpy as np
    import concourse.bacc as bacc
    from concourse.bass_utils import run_bass_kernel_spmd

    ctx = np.asarray(ctx_1024)
    batches, tokens, channels = x.shape
    x_t = np.asarray(x).reshape(batches, tokens, channels // P, P).transpose(3, 0, 2, 1)
    idx = np.asarray(L0_ffn_down_reorder_index)
    hidden = idx.shape[0]
    ends = [min(e, hidden) for e in range(P, hidden + P, P)]
    arrays = {
        "x": np.ascontiguousarray(x),
        "x_t": np.ascontiguousarray(x_t.reshape(P, -1)),
        "ctx_t": np.ascontiguousarray(ctx.transpose(2, 0, 1).reshape(ctx.shape[2], -1)),
        "wqk": np.concatenate([np.asarray(L0_xattn_Wq).T, np.asarray(L0_xattn_Wk).T,
                               np.asarray(L0_xattn_bq)[:, None], np.asarray(L0_xattn_bk)[:, None]], axis=1),
        "w_gate_up": np.concatenate([np.asarray(L0_ffn_w_gate), np.asarray(L0_ffn_w_up)], axis=1),
        "w_down": np.ascontiguousarray(L0_ffn_w_down),
        "down_idx": np.stack([idx[e - P:e] for e in ends], axis=1),
    }
    nc = bacc.Bacc("TRN2", target_bir_lowering=False, num_devices=1)
    aps = [nc.dram_tensor(f"{n}_dram", arrays[n].shape, mybir.dt.from_np(arrays[n].dtype),
                          kind="ExternalInput").ap() for n in _INPUTS]
    out = nc.dram_tensor("out_dram", arrays["x"].shape, F32, kind="ExternalOutput").ap()
    build(nc, *aps, out)
    r = run_bass_kernel_spmd(nc, [{f"{n}_dram": arrays[n] for n in _INPUTS}], core_ids=[0])
    return r.results[0]["out_dram"]
```
